# Optimizing a Trainium2 kernel written in Bass

```python
import numpy as np
import jax
import jax.numpy as jnp

def _softmax(x, axis=-1):
    return jax.nn.softmax(x, axis=axis)

def _gelu(x):
    return jax.nn.gelu(x, approximate=True)

def _silu(x):
    return jax.nn.silu(x)

def _sigmoid(x):
    return jax.nn.sigmoid(x)

def _layernorm(x, axis=-1, eps=1e-05):
    m = jnp.mean(x, axis=axis, keepdims=True)
    v = jnp.var(x, axis=axis, keepdims=True)
    return (x - m) / jnp.sqrt(v + eps)

def _scatter_add(tgt, idx, src, axis=0):
    return tgt.at[idx].add(src)

def _segment_sum(src, seg, n):
    return jax.ops.segment_sum(src, seg, n)
kernel_name = 'mk_xattn_ffn_d1_seqx_r4_383a61'

def setup_inputs(seed: int=0):
    np.random.seed(seed)
    _w = jnp.asarray

    def _rec_inputs():
        import jax
        import jax.numpy as jnp
        _rk = jax.random.key(seed)
        x = -0.0005146 + 1 * jax.random.normal(jax.random.fold_in(_rk, 1), (1, 2048, 256), jnp.float32)
        _lenS = 2048 - jax.random.randint(jax.random.fold_in(_rk, 7), (1,), 0, max(1, 2048 // 4) + 1, jnp.int32)
        _lenS2 = 1601 - jax.random.randint(jax.random.fold_in(_rk, 8), (1,), 0, max(1, 1601 // 4) + 1, jnp.int32)
        _ctx_768P = jax.random.normal(jax.random.fold_in(_rk, 11), (1, 16, 192), jnp.float32)
        _ctx_768c = jax.random.dirichlet(jax.random.fold_in(_rk, 511), 0.3 * jnp.ones((16,), jnp.float32), (1, 1601))
        _ctx_768t = jnp.einsum('bsk,bkd->bsd', _ctx_768c, _ctx_768P)
        _ctx_768t = _ctx_768t * jax.lax.rsqrt(jnp.mean(jnp.square(_ctx_768t)) + 1e-12) * 0.953939
        ctx_768 = -0.00040386 + 0.999972 * (_ctx_768t + 0.3 * jax.random.normal(jax.random.fold_in(_rk, 611), (1, 1601, 192), jnp.float32))
        _validS = jnp.arange(2048)[None, :] < _lenS[:, None]
        _validS2 = jnp.arange(1601)[None, :] < _lenS2[:, None]
        _causal = jnp.tril(jnp.ones((2048, 2048), dtype=bool))
        mask_BxS2_bk0 = jnp.logical_not(jnp.broadcast_to(_validS2[:, :], (1, 1601)))
        return (x, ctx_768, mask_BxS2_bk0)
    x, ctx_768, mask_BxS2_bk0 = _rec_inputs()

    def _L0_xattn_setup():
        import jax, jax.numpy as jnp
        import numpy as np
        DIM_IN, DIM_LAT, DIM_HEAD = (192, 256, 64)
        INNER = max(DIM_LAT, DIM_IN)
        HEADS = INNER // DIM_HEAD
        SCALE = DIM_HEAD ** (-0.5)
        RMS_EPS = 1e-08
        LN_EPS = 1e-05

        def layernorm(x, g, b):
            mu = jnp.mean(x, axis=-1, keepdims=True)
            var = jnp.mean((x - mu) ** 2, axis=-1, keepdims=True)
            return (x - mu) * jax.lax.rsqrt(var + LN_EPS) * g + b

        def rmsnorm(x, gamma):
            norm = jnp.sqrt(jnp.sum(x * x, axis=-1, keepdims=True)) * x.shape[-1] ** (-0.5)
            return x / jnp.maximum(norm, RMS_EPS) * gamma
        key = jax.random.key(seed)
        ks = jax.random.split(key, 12)
        b, n, m = (4, 1024, 128)
        x = jax.random.normal(ks[0], (b, n, DIM_IN), jnp.float32)
        latents = jax.random.normal(ks[1], (b, m, DIM_LAT), jnp.float32)
        mask = jax.random.randint(ks[2], (b, n), 0, 2).astype(bool)
        s = lambda k, sh, fan: jax.random.normal(k, sh, jnp.float32) * fan ** (-0.5)
        return {'x': x, 'latents': latents, 'mask': mask, 'ln_x_g': jnp.ones((DIM_IN,), jnp.float32), 'ln_x_b': jnp.zeros((DIM_IN,), jnp.float32), 'ln_l_g': jnp.ones((DIM_LAT,), jnp.float32), 'ln_l_b': jnp.zeros((DIM_LAT,), jnp.float32), 'qn_g': jnp.ones((DIM_HEAD,), jnp.float32), 'kn_g': jnp.ones((DIM_HEAD,), jnp.float32), 'Wq': s(ks[3], (INNER, DIM_LAT), DIM_LAT), 'Wkv': s(ks[4], (2 * INNER, DIM_IN), DIM_IN), 'Wlkv': s(ks[5], (2 * INNER, DIM_LAT), DIM_LAT), 'Wo': s(ks[6], (DIM_LAT, INNER), INNER), 'bo': jnp.zeros((DIM_LAT,), jnp.float32)}
    _L0_xattn_all = _L0_xattn_setup()
    _L0_xattn_in = {k: v for k, v in _L0_xattn_all.items() if k in ('ln_x_g', 'ln_x_b', 'ln_l_g', 'ln_l_b', 'qn_g', 'kn_g', 'Wq', 'Wkv', 'Wlkv', 'Wo', 'bo')}
    del _L0_xattn_all

    def _L0_ffn_setup():
        import jax, jax.numpy as jnp
        import numpy as np
        E, H, I, K = (8, 256, 512, 2)
        B, S = (4, 512)
        key = jax.random.key(seed)
        k1, k2, k3, k4 = jax.random.split(key, 4)
        x = jax.random.normal(k1, (B, S, H), dtype=jnp.float32)
        router_w = jax.random.uniform(k2, (E, H), dtype=jnp.float32, minval=-1.0, maxval=1.0) / np.sqrt(H).astype(np.float32)
        w13 = jax.random.normal(k3, (E, H, 2 * I), dtype=jnp.float32) * 0.02
        w2 = jax.random.normal(k4, (E, I, H), dtype=jnp.float32) * 0.02
        return {'x': x, 'router_w': router_w, 'w13': w13, 'w2': w2}
    _L0_ffn_all = _L0_ffn_setup()
    _L0_ffn_in = {k: v for k, v in _L0_ffn_all.items() if k in ('router_w', 'w13', 'w2')}
    del _L0_ffn_all
    return {'x': x, 'ctx_768': ctx_768, 'mask_BxS2_bk0': mask_BxS2_bk0, 'L0_xattn_ln_x_g': _L0_xattn_in['ln_x_g'], 'L0_xattn_ln_x_b': _L0_xattn_in['ln_x_b'], 'L0_xattn_ln_l_g': _L0_xattn_in['ln_l_g'], 'L0_xattn_ln_l_b': _L0_xattn_in['ln_l_b'], 'L0_xattn_qn_g': _L0_xattn_in['qn_g'], 'L0_xattn_kn_g': _L0_xattn_in['kn_g'], 'L0_xattn_Wq': _L0_xattn_in['Wq'], 'L0_xattn_Wkv': _L0_xattn_in['Wkv'], 'L0_xattn_Wlkv': _L0_xattn_in['Wlkv'], 'L0_xattn_Wo': _L0_xattn_in['Wo'], 'L0_xattn_bo': _L0_xattn_in['bo'], 'L0_ffn_router_w': _L0_ffn_in['router_w'], 'L0_ffn_w13': _L0_ffn_in['w13'], 'L0_ffn_w2': _L0_ffn_in['w2']}

def reference(x, ctx_768, mask_BxS2_bk0, L0_xattn_ln_x_g, L0_xattn_ln_x_b, L0_xattn_ln_l_g, L0_xattn_ln_l_b, L0_xattn_qn_g, L0_xattn_kn_g, L0_xattn_Wq, L0_xattn_Wkv, L0_xattn_Wlkv, L0_xattn_Wo, L0_xattn_bo, L0_ffn_router_w, L0_ffn_w13, L0_ffn_w2):
    import jax
    import jax.numpy as jnp

    def _L0_xattn_ref(x, latents, mask, ln_x_g, ln_x_b, ln_l_g, ln_l_b, qn_g, kn_g, Wq, Wkv, Wlkv, Wo, bo):
        import jax, jax.numpy as jnp
        import numpy as np
        DIM_IN, DIM_LAT, DIM_HEAD = (192, 256, 64)
        INNER = max(DIM_LAT, DIM_IN)
        HEADS = INNER // DIM_HEAD
        SCALE = DIM_HEAD ** (-0.5)
        RMS_EPS = 1e-08
        LN_EPS = 1e-05

        def layernorm(x, g, b):
            mu = jnp.mean(x, axis=-1, keepdims=True)
            var = jnp.mean((x - mu) ** 2, axis=-1, keepdims=True)
            return (x - mu) * jax.lax.rsqrt(var + LN_EPS) * g + b

        def rmsnorm(x, gamma):
            norm = jnp.sqrt(jnp.sum(x * x, axis=-1, keepdims=True)) * x.shape[-1] ** (-0.5)
            return x / jnp.maximum(norm, RMS_EPS) * gamma
        b, n, _ = x.shape
        m = latents.shape[1]
        xn = layernorm(x, ln_x_g, ln_x_b)
        ln = layernorm(latents, ln_l_g, ln_l_b)
        q = ln @ Wq.T
        kv = jnp.concatenate([xn @ Wkv.T, ln @ Wlkv.T], axis=1)
        k, v = (kv[..., :INNER], kv[..., INNER:])
        split_heads = lambda t: t.reshape(t.shape[0], t.shape[1], HEADS, DIM_HEAD).transpose(0, 2, 1, 3)
        q, k, v = (split_heads(q), split_heads(k), split_heads(v))
        qn = rmsnorm(q, qn_g) * SCALE
        kn = rmsnorm(k, kn_g)
        attn = jnp.einsum('bhid,bhjd->bhij', qn, kn)
        full_mask = jnp.pad(mask, ((0, 0), (0, m)), constant_values=True)
        attn = jnp.where(full_mask[:, None, None, :], attn, -jnp.finfo(attn.dtype).max)
        attn = jax.nn.softmax(attn, axis=-1)
        out = jnp.einsum('bhij,bhjd->bhid', attn, v)
        out = out.transpose(0, 2, 1, 3).reshape(b, m, INNER)
        return out @ Wo.T + bo

    def _L0_ffn_ref(x, router_w, w13, w2):
        import jax, jax.numpy as jnp
        import numpy as np
        E, H, I, K = (8, 256, 512, 2)
        B, S = (4, 512)
        logits = jnp.einsum('bsh,eh->bse', x, router_w)
        probs = jax.nn.softmax(logits, axis=-1)
        weights, indices = jax.lax.top_k(probs, K)
        weights = weights / (weights.sum(axis=-1, keepdims=True) + 1e-06)
        h13 = jnp.einsum('bsh,ehi->bsei', x, w13)
        gate, up = jnp.split(h13, 2, axis=-1)
        h = jax.nn.silu(gate) * up
        y = jnp.einsum('bsei,eih->bseh', h, w2)
        y_sel = jnp.take_along_axis(y, indices[..., None], axis=2)
        return (y_sel * weights[..., None]).sum(axis=2)
    x = x + _L0_xattn_ref(ctx_768, _layernorm(x, axis=-1), mask_BxS2_bk0, L0_xattn_ln_x_g, L0_xattn_ln_x_b, L0_xattn_ln_l_g, L0_xattn_ln_l_b, L0_xattn_qn_g, L0_xattn_kn_g, L0_xattn_Wq, L0_xattn_Wkv, L0_xattn_Wlkv, L0_xattn_Wo, L0_xattn_bo)
    x = x + _L0_ffn_ref(_layernorm(x, axis=-1), L0_ffn_router_w, L0_ffn_w13, L0_ffn_w2)
    return x

_drawn_inputs = setup_inputs


def setup_inputs(seed=0):
    import zlib

    import numpy as np

    out = dict(_drawn_inputs(seed))
    spreads = {'L0_xattn_ln_x_g': (1.0, 0.6),
     'L0_xattn_ln_x_b': (0.0, 0.374),
     'L0_xattn_ln_l_g': (1.0, 0.536),
     'L0_xattn_ln_l_b': (0.0, 0.1),
     'L0_xattn_qn_g': (1.0, 0.6),
     'L0_xattn_kn_g': (1.0, 0.6),
     'L0_xattn_bo': (0.0, 0.1)}
    factors = {'L0_ffn_router_w': 3.806, 'L0_ffn_w13': 3.305, 'L0_ffn_w2': 3.298}
    for name, (base, spread) in spreads.items():
        noise = np.random.default_rng([zlib.crc32(name.encode()), seed]).standard_normal(out[name].shape)
        drawn = base * np.exp(spread * noise) if base else spread * noise
        out[name] = jnp.asarray(drawn.astype(out[name].dtype))
    for name, factor in factors.items():
        out[name] = (out[name] * factor).astype(out[name].dtype)
    return out
```

```python
import concourse.bass as bass
from concourse import mybir
from contextlib import ExitStack

F32 = mybir.dt.float32
F32R = mybir.dt.float32r
I32 = mybir.dt.int32
U32 = mybir.dt.uint32
U8 = mybir.dt.uint8
ALU = mybir.AluOpType
ACT = mybir.ActivationFunctionType
AX = mybir.AxisListType.X

P = 128
TOK, DIM = 2048, 256
CTX, CIN = 1601, 192
H, D = 4, 64
E, I = 8, 512
NT = TOK // P
NC = -(-CTX // P)
NK = NC + NT
KEYS = NK * P
A = D + 2
QB = 4
NB = NT // QB
VW = 2 * D + 1
NP = (NK + 1) // 2
PIECE = 1024
NG = -(-KEYS // PIECE)
NM = QB * NG
ROWS = 2 * TOK
BLK = P
NBLK = (ROWS - E) // BLK + E
EW = (DIM // P) * 2 * I + (I // P) * DIM
WC = 256
BIG = 1e30
SCALE = D ** -0.5
LN_EPS = 1e-5
RMS_EPS = 1e-8


class Step:

    def __init__(self, i, off):
        self.i, self.off = i, off

    @property
    def v(self):
        return self.off if self.i is None else 2 * self.i + self.off

    @property
    def half(self):
        return self.off // 2 if self.i is None else self.i + self.off // 2

    @property
    def par(self):
        return self.off % 2

    def back(self, k):
        return Step(self.i, self.off - k)


def run_steps(eng, lo, hi, body):
    if (hi - lo) % 2 or hi - lo < 4 or lo < 5:
        body(Step(None, lo))
        if hi - lo > 1:
            run_steps(eng, lo + 1, hi, body)
        return
    with eng.Fori(0, (hi - lo) // 2) as i:
        body(Step(i, lo))
        body(Step(i, lo + 1))


def build(nc, x, ctx_in, mask, ln_x_g, ln_x_b, ln_l_g, ln_l_b, qn_g, kn_g, w_lat, w_ctx, wo_t, bo,
          router_t, w13, w2, out):
    xln_d = nc.dram_tensor("xln_d", [TOK, DIM], F32, kind="Internal").ap()
    v_d = nc.dram_tensor("v_d", [H, P, NK, VW], F32, kind="Internal").ap()
    wsp_d = nc.dram_tensor("wsp_d", [E, P, 2, EW], F32, kind="Internal").ap()
    stack = ExitStack()

    def sb(name, shape, dt=F32, at=stack):
        return at.enter_context(nc.sbuf_tensor(name, shape, dt))

    def bank(name, n=1, at=stack):
        return at.enter_context(nc.psum_tensor(name, [P, n, 512], F32))

    with stack:
        names = {}

        def sem(name):
            if name not in names:
                names[name] = stack.enter_context(nc.semaphore(name))
            return names[name]

        ident = sb("ident", [P, P])
        wtab = sb("wtab", [P, NBLK])
        gidx = sb("gidx", [P, NBLK], I32)
        sidx = sb("sidx", [P, NBLK], I32)
        eid = sb("eid", [P, NBLK], I32)
        ring_g = sb("ring_g", [P, 2], I32)
        ring_s = sb("ring_s", [P, 2], I32)
        mcol = sb("mcol", [P, NK])
        cols = sb("cols", [P, 8])
        eps = sb("eps", [P, 1])
        pro = ExitStack()
        ctxt = sb("ctxt", [P, NC, CIN], at=pro)
        knat = sb("knat", [P, 2, H, A], at=pro)
        xn = sb("xn", [P, 2, DIM], at=pro)
        pro.close()
        Ph = sb("Ph", [P, 3, 2, QB * P], F32R, at=pro)
        pro.close()
        xg = sb("xg", [P, 2, DIM])
        xTe = sb("xTe", [P, 2, 2, 2, P], F32R)
        hs = sb("hs", [P, I])
        hTe = sb("hTe", [P, 2, I // P, P], F32R)
        ysb = sb("ysb", [P, 2, DIM])

        big = ExitStack()
        S1 = sb("S1", [P, H, KEYS], F32R, at=big)
        S2 = sb("S2", [P, H, KEYS], F32R, at=big)
        qnat = sb("qnat", [P, QB + H * NT, A], at=big)
        top = ExitStack()
        t0 = ExitStack()
        xall = sb("xall", [P, NT, DIM], at=t0)
        wl = sb("wl", [P, 2, 3 * DIM], at=t0)
        wc = sb("wc", [P, 2, 2 * DIM], at=t0)
        xT = sb("xT", [P, 2, 2, P], at=t0)
        m_u8 = sb("m_u8", [P, NC], U8, at=t0)
        gq = sb("gq", [P, 2, D], at=t0)
        gs = sb("gs", [P, D], at=t0)
        mvs = sb("mvs", [P, NK, 2], at=t0)
        st6 = sb("st6", [P, NK, 6], at=t0)
        rsd = sb("rsd", [P, NK], at=t0)
        sda = sb("sda", [P, NK], at=t0)
        va = sb("va", [P, NK], at=t0)
        ss = sb("ss", [P, 2 * H], at=t0)
        nrm = sb("nrm", [P, 2 * H], at=t0)
        rn0 = sb("rn0", [P, 2 * H], at=t0)
        rn = sb("rn", [P, 2 * H], at=t0)
        Vs = sb("Vs", [P, 2, H, VW], F32R, at=t0)
        t0.close()
        t1 = ExitStack()
        V = sb("V", [P, 2, NK, VW], F32R, at=t1)
        Q1 = sb("Q1", [P, 2, QB * P], F32R, at=t1)
        Q2 = sb("Q2", [P, 2, QB * P], F32R, at=t1)
        part = ExitStack()
        PT = sb("PT", [P, 3, 2, QB * P], at=part)
        part.close()
        Pl = sb("Pl", [P, 3, 2, QB * P], F32R, at=t1)
        qst = sb("qst", [P, QB, A], at=t1)
        wraw = sb("wraw", [P, 2, WC], at=t1)
        whi = sb("whi", [P, 2, WC], F32R, at=t1)
        oT_a = sb("oT_a", [P, QB * P], at=t1)
        mpart = sb("mpart", [P, QB, NG], at=t1)
        cmax = sb("cmax", [P, QB], at=t1)
        orec = sb("orec", [P, QB], at=t1)
        t1.close()
        top.close()
        t2 = ExitStack()
        wot = sb("wot", [P, 2, DIM], at=t2)
        rt = sb("rt", [P, 2, E], at=t2)
        bob = sb("bob", [P, DIM], at=t2)
        ost = sb("ost", [P, 2, DIM], at=t2)
        oT = sb("oT", [P, 2, 2, P], at=t2)
        xin = sb("xin", [P, 2, DIM], at=t2)
        x2 = sb("x2", [P, 2, DIM], at=t2)
        x3 = sb("x3", [P, 2, DIM], at=t2)
        x3T = sb("x3T", [P, 2, 2, P], at=t2)
        st2 = sb("st2", [P, 6], at=t2)
        mv2 = sb("mv2", [P, 2], at=t2)
        sd2 = sb("sd2", [P, 1], at=t2)
        rs2 = sb("rs2", [P, 1], at=t2)
        lg = sb("lg", [P, NT, E], at=t2)
        zrow = sb("zrow", [P, DIM], at=t2)
        iot_i = sb("iot_i", [P, P], I32, at=t2)
        iot = sb("iot", [P, P], at=t2)
        tid_i = sb("tid_i", [P, NT], I32, at=t2)
        tid = sb("tid", [P, NT], at=t2)
        pc_i = sb("pc_i", [P, 1], I32, at=t2)
        pc = sb("pc", [P, 1], at=t2)
        U = sb("U", [P, P], at=t2)
        ones = sb("ones", [P, P], at=t2)
        thr = sb("thr", [P, NBLK + 1], at=t2)
        w8 = sb("w8", [P, E], at=t2)
        ra = sb("ra", [P, NT, E], at=t2)
        rb = sb("rb", [P, NT, E], at=t2)
        pr = sb("pr", [P, NT, E], at=t2)
        oh = sb("oh", [P, 2, NT, E], at=t2)
        M = sb("M", [P, NT, E], at=t2)
        tot = sb("tot", [P, NT, E], at=t2)
        top_p = sb("top_p", [P, 2, NT], at=t2)
        sm = sb("sm", [P, NT], at=t2)
        wgt = sb("wgt", [P, 2, NT], at=t2)
        pos = sb("pos", [P, 2, NT], at=t2)
        rr = sb("rr", [P, 2, NT], at=t2)
        cmp8 = sb("cmp8", [P, E, NT], at=t2)
        nb = sb("nb", [P, E], at=t2)
        cs = sb("cs", [P, 2, E], at=t2)
        st128 = sb("st128", [P, E], at=t2)
        G = sb("G", [P, 2 * NT, NBLK + 1], at=t2)
        mov = sb("mov", [P, 2 * NT, 2, NBLK], at=t2)
        ohr = sb("ohr", [P, 2 * NT, P], at=t2)
        ecmp = sb("ecmp", [P, NBLK, E - 1], at=t2)
        ef = sb("ef", [P, NBLK], at=t2)
        tok = sb("tok", [P, NBLK], at=t2)
        zt = sb("zt", [P, NBLK], at=t2)
        t2.close()
        big.close()
        W = sb("W", [P, E, 2, EW], F32R)

        ph = ExitStack()
        bX = [bank(f"bX{i}", at=ph) for i in range(2)]
        bA = [bank(f"bA{i}", at=ph) for i in range(2)]
        bV = [bank(f"bV{i}", at=ph) for i in range(2)]
        bK = bank("bK", at=ph)
        bSq = bank("bSq", at=ph)
        ph.close()
        bS = [bank(f"bS{i}", 2, at=ph) for i in range(2)]
        bM = bank("bM", 2, at=ph)
        bPV = bank("bPV", at=ph)
        bT = bank("bT", at=ph)
        ph.close()
        bFT = [bank(f"bFT{i}", at=ph) for i in range(2)]
        bFY = [bank(f"bFY{i}", at=ph) for i in range(2)]
        bFX = [bank(f"bFX{i}", at=ph) for i in range(2)]
        bL = bank("bL", at=ph)
        bR = bank("bR", at=ph)
        ph.close()
        bG = [bank(f"bG{i}", at=ph) for i in range(2)]
        bU = [bank(f"bU{i}", at=ph) for i in range(2)]
        bXe = bank("bXe", at=ph)
        bH = bank("bH", at=ph)
        bY = bank("bY", at=ph)
        ph.close()

        block = stack.enter_context(nc.Block())

        q_by_head = qnat[:, QB:, :].rearrange("p (h t) a -> p h t a", t=NT)

        def heads(ap, lo=0, n=D):
            return ap.rearrange("p (h d) -> p h d", h=ap.shape[1] // n)

        @block.sync
        def _(sp):
            for n, (lo, hi) in enumerate(CTX_LOADS):
                sp.dma_start(ctxt[:, lo:hi, :], ctx_in[lo * P:hi * P, :].rearrange("(t p) d -> p t d", p=P))\
                    .then_inc(sem(f"ctx_in{n}"), 16)
            sp.wait_ge(sem("ctx_pad"), 1)
            sp.dma_start(ctxt[0:CTX - (NC - 1) * P, NC - 1, :], ctx_in[(NC - 1) * P:CTX, :])\
                .then_inc(sem("ctx_in_l"), 16)
            sp.dma_start(xall[:], x.rearrange("(t p) d -> p t d", p=P)).then_inc(sem("x_in"), 16)
            sp.dma_start(wl[:], w_lat.rearrange("(k p) n -> p k n", p=P)).then_inc(sem("wl_in"), 16)

            def v_store(s):
                sp.wait_ge(sem("v_lo"), s.v + 1)
                sp.dma_start(v_d[:, :, s.v, :].rearrange("h p c -> p h c"), Vs[:, s.par, :, :].bitcast(F32))\
                    .then_inc(sem(f"v_st{s.par}"), 16)

            run_steps(sp, 0, NK, v_store)

            def v_load(h):
                sp.dma_start(V[:, h % 2, :, :].bitcast(F32), v_d[h]).then_inc(sem(f"v_in{h % 2}"), 16)

            for j in range(2):
                sp.wait_ge(sem(f"v_st{j}"), (NK + 1 - j) // 2 * 16)
            sp.wait_ge(sem("klo"), NK)
            sp.wait_ge(sem("s1"), NK)
            sp.wait_ge(sem("q_s"), NT)
            v_load(0)
            v_load(1)
            NCH = EW // WC

            def src(e, ch):
                n13 = (DIM // P) * 2 * I // WC
                if ch < n13:
                    k, c = divmod(ch * WC, 2 * I)
                    return w13[e, k * P:(k + 1) * P, c:c + WC]
                k = (ch - n13) * WC // DIM
                return w2[e, k * P:(k + WC // DIM) * P, :].rearrange("(k p) n -> p k n", p=P)

            def load(e, ch):
                dst = wraw[:, ch % 2, :]
                if ch * WC >= (DIM // P) * 2 * I:
                    dst = dst.rearrange("p (k n) -> p k n", n=DIM)
                sp.dma_start(dst, src(e, ch)).then_inc(sem(f"raw{ch % 2}"), 16)

            load(0, 0)
            load(0, 1)

            def store(e, i, ch):
                sp.wait_ge(sem("wsplit"), NCH * i + ch + 1)
                for part, buf in enumerate((whi[:, ch % 2, :].bitcast(F32), wraw[:, ch % 2, :])):
                    sp.dma_start(wsp_d[e, :, part, ch * WC:(ch + 1) * WC], buf).then_inc(sem(f"wst{ch % 2}"), 16)
                sp.wait_ge(sem(f"wst{ch % 2}"), 32 * (NCH // 2 * i + ch // 2) + 32)

            with sp.Fori(0, E - 1) as e:
                for ch in range(NCH):
                    store(e, e, ch)
                    load(e + (ch + 2) // NCH, (ch + 2) % NCH)
            for ch in range(NCH):
                store(E - 1, E - 1, ch)
                if ch + 2 < NCH:
                    load(E - 1, ch + 2)
            for h in range(2, H):
                sp.wait_ge(sem("pv"), 3 + NP * NB * (h - 1))
                v_load(h)

            sp.wait_ge(sem("o_ev"), UNITS + 1)
            sp.dma_start(bob[:], bo.partition_broadcast(P)).then_inc(sem("c_bo"), 16)
            sp.dma_start(wot[:], wo_t.rearrange("(k p) n -> p k n", p=P)).then_inc(sem("c_wo"), 16)
            sp.dma_start(rt[:], router_t.rearrange("(k p) n -> p k n", p=P)).then_inc(sem("c_rt"), 16)
            xt = x.rearrange("(t p) d -> t p d", p=P)
            ot = out[0:TOK, :].rearrange("(t p) d -> t p d", p=P)
            xlt = xln_d.rearrange("(t p) d -> t p d", p=P)

            def load_x(s):
                sp.dma_start(xin[:, s.par, :], xt[s.v, :, :]).then_inc(sem(f"xin{s.par}"), 16)

            def io(s, more):
                sp.wait_ge(sem("x2"), s.v + 1)
                sp.dma_start(ot[s.v, :, :], x2[:, s.par, :]).then_inc(sem(f"ox{s.par}"), 16)
                if more:
                    load_x(s.back(-2))
                sp.wait_ge(sem("x3"), s.v + 1)
                sp.dma_start(xlt[s.v, :, :], x3[:, s.par, :]).then_inc(sem(f"ol{s.par}"), 16)

            load_x(Step(None, 0))
            load_x(Step(None, 1))
            run_steps(sp, 0, NT - 2, lambda s: io(s, True))
            for t in (NT - 2, NT - 1):
                io(Step(None, t), False)
            sp.wait_ge(sem("zrow"), 1)
            sp.dma_start(out[TOK:TOK + BLK, :], zrow[:]).then_inc(sem("pad_out"), 16)
            for j in range(2):
                sp.wait_ge(sem(f"ox{j}"), NT // 2 * 16)
                sp.wait_ge(sem(f"ol{j}"), NT // 2 * 16)
            sp.wait_ge(sem("pad_out"), 16)
            sp.sem_inc(sem("rows_out"), 1)
            for e in range(E):
                if e == 4:
                    sp.wait_ge(sem("routed"), 1)
                sp.dma_start(W[:, e, :, :].bitcast(F32), wsp_d[e, :, :, :]).then_inc(sem(f"we{e % 2}"), 16)
                if e:
                    sp.wait_ge(sem(f"we{(e - 1) % 2}"), (e + 1) // 2 * 16)
                    sp.sem_inc(sem("w_in"), 1)
            sp.wait_ge(sem(f"we{(E - 1) % 2}"), E // 2 * 16)
            sp.sem_inc(sem("w_in"), 1)

        @block.gpsimd
        def _(pool):
            def held():
                pool.sem_inc(sem("pool_held"), 1)

            pool.memset(ident[:], 0.0).then_inc(sem("id0"), 1)
            pool.memset(ctxt[:, NC - 1, :], 0.0).then_inc(sem("ctx_pad"), 1)
            pool.memset(mcol[:], 0.0).then_inc(sem("mc0"), 1)
            pool.wait_ge(sem("id0"), 1)
            pool.affine_select(out=ident[:], in_=ident[:], compare_op=ALU.not_equal, fill=1.0, base=0,
                               pattern=[[-1, P]], channel_multiplier=1).then_inc(sem("ident"), 1)
            pool.memset(knat[:, :, :, D:D + 1], -1.0).then_inc(sem("kn0"), 1)
            pool.memset(Vs[:, :, :, D:D + 1].bitcast(F32), 1.0).then_inc(sem("v1"), 1)
            pool.memset(qnat[:, :, D:D + 1], 0.0).then_inc(sem("qn0"), 1)
            pool.memset(qnat[:, :, D + 1:D + 2], 1.0).then_inc(sem("qn0"), 1)
            pool.wait_ge(sem("ident"), 1)
            pool.wait_ge(sem("ctx_pad"), 1)
            pool.wait_ge(sem("mc0"), 1)
            pool.wait_ge(sem("kn0"), 1)
            pool.wait_ge(sem("v1"), 1)
            pool.wait_ge(sem("qn0"), 2)
            pool.memset(S2[D:P, :, :].bitcast(F32), 0.0).then_inc(sem("s20"), 1)
            pool.wait_ge(sem("s20"), 1)

            def pro(s, mk, qs):
                if mk:
                    t = s.back(1)
                    if not (t.i is None and t.off < 2):
                        pool.wait_ge(sem("kT_mm"), t.v - 1)
                    pool.wait_ge(sem("mcol"), 1)
                    held()
                    pool.tensor_copy(knat[:, t.par, :, D + 1], mcol[:, bass.ds(t.v, 1)].to_broadcast([P, H]))\
                        .then_inc(sem("kmask"), 1)
                if qs:
                    t = s.back(1 + NC)
                    pool.wait_ge(sem("q_n"), t.v + 1)
                    pool.tensor_tensor(q_by_head[:, :, t.v, 0:D], q_by_head[:, :, t.v, 0:D],
                                       gs[:].unsqueeze(1).to_broadcast([P, H, D]), ALU.mult)\
                        .then_inc(sem("q_s"), 1)

            for lo, hi, a in ((1, NC + 1, (1, 0)), (NC + 1, NK + 1, (1, 1))):
                run_steps(pool, lo, hi, lambda s, a=a: pro(s, *a))

            NCH = EW // WC

            def split(i, ch):
                n = NCH * i + ch
                half = NCH // 2 * i + ch // 2
                pool.wait_ge(sem(f"raw{ch % 2}"), 16 * half + 16)
                return n, half

            def split_body(i, ch, first):
                n, half = split(i, ch)
                if not first:
                    pool.wait_ge(sem(f"wst{ch % 2}"), 32 * half)
                held()
                pool.tensor_copy(whi[:, ch % 2, :], wraw[:, ch % 2, :]).then_inc(sem("whi"), 1)
                pool.wait_ge(sem("whi"), n + 1)
                pool.tensor_tensor(wraw[:, ch % 2, :].bitcast(F32R), wraw[:, ch % 2, :], whi[:, ch % 2, :].bitcast(F32),
                                   ALU.subtract).then_inc(sem("wsplit"), 1)

            for ch in range(NCH):
                split_body(0, ch, ch < 2)
            with pool.Fori(1, E) as e:
                for ch in range(NCH):
                    split_body(e, ch, False)

            pool.wait_ge(sem("o_ev"), UNITS + 1)
            pool.wait_ge(sem("wst0"), E * NCH // 2 * 32)
            pool.wait_ge(sem("wst1"), E * NCH // 2 * 32)
            pool.memset(zrow[:], 0.0).then_inc(sem("zrow"), 1)
            pool.iota(iot_i[:], pattern=[[1, P]], base=0, channel_multiplier=0).then_inc(sem("iota"), 1)
            pool.iota(tid_i[:], pattern=[[P, NT]], base=1, channel_multiplier=1).then_inc(sem("iota"), 1)
            pool.iota(pc_i[:], pattern=[[0, 1]], base=TOK + 1, channel_multiplier=1).then_inc(sem("iota"), 1)
            pool.memset(ones[:], 1.0).then_inc(sem("ones"), 1)
            pool.memset(U[:], 1.0).then_inc(sem("u0"), 1)
            pool.wait_ge(sem("u0"), 1)
            pool.affine_select(out=U[:], in_=U[:], compare_op=ALU.is_gt, fill=0.0, base=0,
                               pattern=[[1, P]], channel_multiplier=-1).then_inc(sem("U"), 1)

            pool.wait_ge(sem("routed"), 1)
            pool.wait_ge(sem("rows_out"), 1)

            def gather(s):
                if not (s.i is None and s.off < 2):
                    pool.wait_ge(sem("xTe_mm"), s.v - 1)
                    pool.wait_ge(sem(f"g_in{s.par}"), 16 * s.half)
                held()
                pool.tensor_copy(ring_g[:, s.par:s.par + 1], gidx[:, bass.ds(s.v, 1)]).then_inc(sem("rg"), 1)
                pool.wait_ge(sem("rg"), s.v + 1)
                held()
                pool.indirect_dma_start(xg[:, s.par, :], None, xln_d,
                                        bass.IndirectOffsetOnAxis(ap=ring_g[:, s.par:s.par + 1], axis=0))\
                    .then_inc(sem(f"g_in{s.par}"), 16)

            def scatter(s):
                pool.wait_ge(sem("ysb"), s.v + 1)
                if not (s.i is None and s.off < 2):
                    pool.wait_ge(sem(f"add{s.par}"), 16 * s.half)
                held()
                pool.tensor_copy(ring_s[:, s.par:s.par + 1], sidx[:, bass.ds(s.v, 1)]).then_inc(sem("rs"), 1)
                pool.wait_ge(sem("rs"), s.v + 1)
                if not (s.i is None and s.off < 1):
                    b = s.back(1)
                    pool.wait_ge(sem(f"add{b.par}"), 16 * b.half + 16)
                held()
                pool.indirect_dma_start(out, bass.IndirectOffsetOnAxis(ap=ring_s[:, s.par:s.par + 1], axis=0),
                                        ysb[:, s.par, :], None, compute_op=ALU.add)\
                    .then_inc(sem(f"add{s.par}"), 16)

            def step(s, g, sc):
                if g:
                    gather(s)
                if sc:
                    scatter(s.back(3))

            for lo, hi, a in ((0, 3, (1, 0)), (3, NBLK, (1, 1)), (NBLK, NBLK + 3, (0, 1))):
                run_steps(pool, lo, hi, lambda s, a=a: step(s, *a))
            for j in range(2):
                pool.wait_ge(sem(f"add{j}"), 16 * ((NBLK + 1 - j) // 2))

        @block.scalar
        def _(act):
            act.dma_start(wc[0:P, 0, :], w_ctx[0:P, :]).then_inc(sem("wc_in"), 16)
            act.dma_start(wc[0:CIN - P, 1, :], w_ctx[P:CIN, :]).then_inc(sem("wc_in2"), 16)
            gains = ((ln_x_g, CIN), (ln_x_b, CIN), (ln_l_g, DIM), (ln_l_b, DIM))
            for n, (g, w) in enumerate(gains):
                for k in range(2):
                    r = min(P, w - k * P)
                    act.dma_start(cols[0:r, 2 * n + k:2 * n + k + 1],
                                  g[k * P:k * P + r].rearrange("(p a) -> p a", a=1)).then_inc(sem("cols"), 16)
            act.dma_start(gq[:, 0, :], qn_g.partition_broadcast(P)).then_inc(sem("gq"), 16)
            act.dma_start(gq[:, 1, :], kn_g.partition_broadcast(P)).then_inc(sem("gq"), 16)
            act.dma_start(m_u8[:, 0:NC - 1], mask[0:(NC - 1) * P].rearrange("(t p) -> p t", p=P),
                          allow_slow_non_contiguous=True).then_inc(sem("m_in"), 16)
            act.dma_start(m_u8[0:CTX - (NC - 1) * P, NC - 1:NC],
                          mask[(NC - 1) * P:CTX].rearrange("(p a) -> p a", a=1)).then_inc(sem("m_in"), 16)

            act.wait_ge(sem("bn"), NC)
            act.activation(sda[:, 0:NC], mvs[:, 0:NC, 1], ACT.Sqrt, bias=eps[:, 0:1]).then_inc(sem("sd_c"), 1)

            def pro(s, b, c):
                if b:
                    t = s.back(2)
                    lo = 0 if b == 'l' else DIM
                    act.wait_ge(sem("qk_mm"), t.v + 1)
                    if not (t.i is None and t.off < 1):
                        act.wait_ge(sem("ss"), t.v)
                    act.activation(bSq[:, 0, lo:2 * DIM], bA[t.par][:, 0, lo:2 * DIM], ACT.Square)\
                        .then_inc(sem("sq"), 1)
                kT = bK[0:A, 0, :].rearrange("p (h c) -> p h c", h=H)
                if c:
                    c_ = s.back(3)
                    act.wait_ge(sem("kT_mm"), c_.v + 1)
                    act.copy(S2[0:A, :, bass.ds(c_.v * P, P)], kT).then_inc(sem("s2"), 1)
                if b:
                    act.wait_ge(sem("v_mm"), t.v + 1)
                    if not (t.i is None and t.off < 2):
                        act.wait_ge(sem(f"v_st{t.par}"), 16 * t.half)
                    act.copy(Vs[:, t.par, :, 0:D], heads(bV[t.par][:, 0, 0:DIM])).then_inc(sem("v_hi"), 1)
                    lo = 0 if b == 'l' else H
                    act.wait_ge(sem("ss"), t.v + 1)
                    act.activation(nrm[:, lo:2 * H], ss[:, lo:2 * H], ACT.Sqrt, scale=1.0 / D)\
                        .then_inc(sem("nrm"), 1)
                if c:
                    act.wait_ge(sem("s2"), c_.v + 1)
                    act.copy(S1[0:D, :, bass.ds(c_.v * P, P)],
                             S2[0:D, :, bass.ds(c_.v * P, P)].bitcast(F32)).then_inc(sem("s1"), 1)

            def lat_sd():
                act.wait_ge(sem("bn"), NK)
                act.activation(sda[:, NC:NK], mvs[:, NC:NK, 1], ACT.Sqrt, bias=eps[:, 0:1]).then_inc(sem("sd_l"), 1)
                act.wait_ge(sem("v2"), 1)
                act.activation(sda[:, NC:NK], va[:, NC:NK], ACT.Sqrt, bias=eps[:, 0:1]).then_inc(sem("sd_l"), 1)

            act.wait_ge(sem("v1"), 1)
            act.wait_ge(sem("s20"), 1)
            run_steps(act, 2, 3, lambda s: pro(s, 'c', 0))
            run_steps(act, 3, LAT_AT + 2, lambda s: pro(s, 'c', 1))
            lat_sd()
            for lo, hi, a in ((LAT_AT + 2, NC + 2, ('c', 1)), (NC + 2, NK + 2, ('l', 1)), (NK + 2, NK + 3, (0, 1))):
                run_steps(act, lo, hi, lambda s, a=a: pro(s, *a))

            act.sem_inc(sem("exp"), 2)
            act.wait_ge(sem("klo"), NK)
            act.wait_ge(sem("q_s"), NT)
            act.wait_ge(sem("q1w"), 1)
            act.wait_ge(sem("q20"), 1)

            def q_evac(v, par):
                act.wait_ge(sem("qT_mm"), v + 1)
                act.copy(Q2[0:A, par, :], bT[0:A, 0, :]).then_inc(sem("q2"), 1)
                act.copy(Q1[D:2 * D, par, :], bT[0:D, 0, :]).then_inc(sem("q1h"), 1)

            def c_row(v, par):
                act.wait_ge(sem("cT_mm"), v + 1)
                act.copy(Q2[D:D + 1, par, :], bT[0:1, 0, :]).then_inc(sem("c_row"), 1)

            def unit(u, j):
                for p in range(NP):
                    g = NP * u + p
                    w = 2 if 2 * p + 1 < NK else 1
                    sl = (NP * j + p) % 2
                    act.wait_ge(sem("s_mm"), g + 1)
                    act.wait_ge(sem("pv"), g + 1)
                    act.activation(PT[:, p % 3, 0:w, :], bS[sl][:, 0:w, :], ACT.Exp).then_inc(sem("exp"), 1)
                    act.wait_ge(sem("exp"), g + 3)
                    act.copy(Ph[:, p % 3, 0:w, :], PT[:, p % 3, 0:w, :]).then_inc(sem("p_hi"), 1)
                    if p == 0:
                        q_evac(u + 1, (j + 1) % 2)
                c_row(u + 1, (j + 1) % 2)
                act.wait_ge(sem("pv"), NP * (u + 1) + 3)
                act.wait_ge(sem("oT_a"), u + 1)
                act.copy(oT_a[0:D + 1, :], bPV[0:D + 1, 0, :]).then_inc(sem("o_cp"), 1)

            q_evac(0, 0)
            c_row(0, 0)
            for h in range(H):
                with act.Fori(0, NB // 2) as i:
                    for j in range(2):
                        unit(NB * h + 2 * i + j, j)

            def fin(s, a, b, c):
                if a:
                    act.wait_ge(sem("oT_mm"), s.v + 1)
                    if not (s.i is None and s.off < 2):
                        act.wait_ge(sem("y_mm"), s.v - 1)
                    act.copy(oT[:, s.par, :, :], bFT[s.par][:, 0, 0:DIM].rearrange("p (k c) -> p k c", k=2))\
                        .then_inc(sem("oT"), 1)
                if b:
                    t = s.back(1)
                    act.wait_ge(sem("mv2"), t.v + 1)
                    act.activation(sd2[:], mv2[:, 1:2], ACT.Sqrt, bias=eps[:, 0:1]).then_inc(sem("sd2"), 1)
                if c:
                    t = s.back(2)
                    act.wait_ge(sem("x3T_mm"), t.v + 1)
                    if not (t.i is None and t.off < 2):
                        act.wait_ge(sem("lg_mm"), t.v - 1)
                    act.copy(x3T[:, t.par, :, :], bFX[t.par][:, 0, 0:DIM].rearrange("p (k c) -> p k c", k=2))\
                        .then_inc(sem("x3T"), 1)

            for lo, hi, a in ((0, 1, (1, 0, 0)), (1, 2, (1, 1, 0)), (2, NT, (1, 1, 1)), (NT, NT + 1, (0, 1, 1)),
                              (NT + 1, NT + 2, (0, 0, 1))):
                run_steps(act, lo, hi, lambda s, a=a: fin(s, *a))
            act.wait_ge(sem("r_sh"), 1)
            act.activation(ra[:], rb[:], ACT.Exp).then_inc(sem("r_ex"), 1)

            def ffn(s, x_, g, h):
                if h:
                    t = s.back(2)
                    act.wait_ge(sem("hT_mm"), t.v + 1)
                    if not (t.i is None and t.off < 1):
                        act.wait_ge(sem("y_e"), t.v)
                    act.copy(hTe[:, 0, :, :], bH[:, 0, :].rearrange("p (k c) -> p k c", k=I // P))\
                        .then_inc(sem("hhi"), 1)
                if g:
                    t = s.back(1)
                    act.wait_ge(sem("g_mm"), t.v + 1)
                    if not (t.i is None and t.off < 1):
                        act.wait_ge(sem("hT_mm"), t.v)
                    act.activation(hs[:], bG[t.par][:, 0, :], ACT.Silu).then_inc(sem("silu"), 1)
                if x_:
                    act.wait_ge(sem("xTe_mm"), s.v + 1)
                    if not (s.i is None and s.off < 2):
                        act.wait_ge(sem("u_mm"), s.v - 1)
                    act.copy(xTe[:, s.par, 0, :, :], bXe[:, 0, 0:DIM].rearrange("p (k c) -> p k c", k=2))\
                        .then_inc(sem("xhi"), 1)

            for lo, hi, a in FFN_SEGMENTS:
                run_steps(act, lo, hi, lambda s, a=a: ffn(s, *a))

        @block.vector
        def _(dve):
            link_n = [0]

            def link(ins):
                link_n[0] += 1
                ins.then_inc(sem("link"), 1)
                dve.wait_ge(sem("link"), link_n[0])

            dve.memset(eps[:], LN_EPS).then_inc(sem("eps"), 1)
            dve.memset(xT[CIN - P:P, :, 1, :], 0.0).then_inc(sem("xT0"), 1)
            dve.memset(wc[CIN - P:P, 1, :], 0.0).then_inc(sem("wc0"), 1)
            dve.wait_ge(sem("m_in"), 32)
            dve.wait_ge(sem("mc0"), 1)
            NF = NC - 1
            link(dve.tensor_scalar(mcol[:, 0:NF], m_u8[:, 0:NF], -1.0, BIG, ALU.add, ALU.mult))
            link(dve.memset(mcol[:, NF:NC], -BIG))
            dve.tensor_scalar(mcol[0:CTX - NF * P, NF:NC], m_u8[0:CTX - NF * P, NF:NC], -1.0, BIG, ALU.add, ALU.mult)\
                .then_inc(sem("mcol"), 1)
            dve.wait_ge(sem("gq"), 32)
            dve.scalar_tensor_tensor(gs[:], gq[:, 0, :], SCALE, gq[:, 1, :], ALU.mult, ALU.mult)\
                .then_inc(sem("gs"), 1)
            def stats(src, t):
                dve.bn_stats(st6[:, t, :], src).then_inc(sem("bn0"), 1)

            def aggregate(lo, hi):
                for t in range(lo, hi):
                    dve.wait_ge(sem("bn0"), t + 1)
                    dve.bn_aggr(mvs[:, t, :], st6[:, t, :]).then_inc(sem("bn"), 1)

            for n, (lo, hi) in enumerate(CTX_LOADS):
                dve.wait_ge(sem(f"ctx_in{n}"), 16)
                for t in range(lo, hi):
                    stats(ctxt[:, t, :], t)
            dve.wait_ge(sem("ctx_in_l"), 16)
            stats(ctxt[:, NC - 1, :], NC - 1)
            aggregate(0, NC)
            dve.wait_ge(sem("sd_c"), 1)
            link(dve.reciprocal(rsd[:, 0:NC], sda[:, 0:NC]))

            def apply(t, kind):
                src = ctxt[:, t.v, :] if kind == 'c' else xall[:, t.back(NC).v, :]
                w = CIN if kind == 'c' else DIM
                if not (t.i is None and t.off < 2):
                    dve.wait_ge(sem("xT_mm"), t.v - 1)
                dve.tensor_scalar(xn[:, t.par, 0:w], src, mvs[:, t.v, 0:1], rsd[:, bass.ds(t.v, 1)],
                                  ALU.subtract, ALU.mult).then_inc(sem("ln"), 1)

            def pro(s, a, ln, b, c):
                if a:
                    dve.wait_ge(sem("xT_mm"), s.v + 1)
                    if not (s.i is None and s.off < 2):
                        dve.wait_ge(sem("v_mm"), s.v - 1)
                    for k in range(2):
                        r = P if (k == 0 or a == 'l') else CIN - P
                        g0 = 0 if a == 'c' else 4
                        dve.tensor_scalar(xT[0:r, s.par, k, :], bX[s.par][0:r, 0, k * P:(k + 1) * P],
                                          cols[0:r, g0 + k:g0 + k + 1], cols[0:r, g0 + 2 + k:g0 + 3 + k],
                                          ALU.mult, ALU.add).then_inc(sem("xT"), 1)
                if ln:
                    apply(s.back(-1), ln)
                if b:
                    t = s.back(2)
                    lo = 0 if b == 'l' else H
                    dve.wait_ge(sem("sq"), t.v + 1)
                    dve.tensor_reduce(ss[:, lo:2 * H], heads(bSq[:, 0, lo * D:2 * DIM]), AX, ALU.add)\
                        .then_inc(sem("ss"), 1)
                if c:
                    c_ = s.back(3)
                    dve.wait_ge(sem("s2"), c_.v + 1)
                    dve.tensor_tensor(S1[D:2 * D, :, bass.ds(c_.v * P, P)],
                                      bK[0:D, 0, :].rearrange("p (h c) -> p h c", h=H),
                                      S2[0:D, :, bass.ds(c_.v * P, P)].bitcast(F32), ALU.subtract)\
                        .then_inc(sem("klo"), 1)
                if b:
                    dve.wait_ge(sem("v_hi"), t.v + 1)
                    dve.tensor_tensor(Vs[:, t.par, :, D + 1:VW], heads(bV[t.par][:, 0, 0:DIM]),
                                      Vs[:, t.par, :, 0:D].bitcast(F32), ALU.subtract).then_inc(sem("v_lo"), 1)
                    dve.wait_ge(sem("nrm"), t.v + 1)
                    dve.tensor_scalar(rn0[:, lo:2 * H], nrm[:, lo:2 * H], RMS_EPS, None, ALU.max)\
                        .then_inc(sem("rn0"), 1)
                    dve.wait_ge(sem("rn0"), t.v + 1)
                    dve.reciprocal(rn[:, lo:2 * H], rn0[:, lo:2 * H]).then_inc(sem("rn"), 1)
                    dve.wait_ge(sem("rn"), t.v + 1)
                    if b == 'l':
                        dve.tensor_tensor(q_by_head[:, :, t.back(NC).v, 0:D], heads(bA[t.par][:, 0, 0:DIM]),
                                          rn[:, 0:H].unsqueeze(2).to_broadcast([P, H, D]), ALU.mult)\
                            .then_inc(sem("q_n"), 1)
                    if not (t.i is None and t.off < 2):
                        dve.wait_ge(sem("kT_mm"), t.v - 1)
                    dve.tensor_tensor(knat[:, t.par, :, 0:D], heads(bA[t.par][:, 0, DIM:2 * DIM]),
                                      rn[:, H:2 * H].unsqueeze(2).to_broadcast([P, H, D]), ALU.mult)\
                        .then_inc(sem("knat"), 1)

            dve.wait_ge(sem("cols"), 128)
            apply(Step(None, 0), 'c')
            dve.wait_ge(sem("xT0"), 1)
            dve.wait_ge(sem("v1"), 1)
            run_steps(dve, 0, 2, lambda s: pro(s, 'c', 'c', 0, 0))
            run_steps(dve, 2, 3, lambda s: pro(s, 'c', 'c', 'c', 0))
            run_steps(dve, 3, LAT_AT + 1, lambda s: pro(s, 'c', 'c', 'c', 1))
            dve.wait_ge(sem("x_in"), 16)
            for t in range(NT):
                stats(xall[:, t, :], NC + t)
            aggregate(NC, NK)
            run_steps(dve, LAT_AT + 1, LAT_AT + 2, lambda s: pro(s, 'c', 'c', 'c', 1))
            L = slice(NC, NK)
            dve.wait_ge(sem("sd_l"), 1)
            link(dve.reciprocal(rsd[:, L], sda[:, L]))
            link(dve.tensor_tensor(va[:, L], rsd[:, L], rsd[:, L], ALU.mult))
            dve.tensor_tensor(va[:, L], va[:, L], mvs[:, L, 1], ALU.mult).then_inc(sem("v2"), 1)
            dve.wait_ge(sem("sd_l"), 2)
            link(dve.reciprocal(va[:, L], sda[:, L]))
            link(dve.tensor_tensor(rsd[:, L], rsd[:, L], va[:, L], ALU.mult))
            for lo, hi, a in ((LAT_AT + 2, NC - 1, ('c', 'c', 'c', 1)), (NC - 1, NC, ('c', 'l', 'c', 1)),
                              (NC, NC + 2, ('l', 'l', 'c', 1)), (NC + 2, NK - 1, ('l', 'l', 'l', 1)),
                              (NK - 1, NK, ('l', 0, 'l', 1)), (NK, NK + 2, (0, 0, 'l', 1)),
                              (NK + 2, NK + 3, (0, 0, 0, 1))):
                run_steps(dve, lo, hi, lambda s, a=a: pro(s, *a))

            dve.wait_ge(sem("q_s"), NT)
            dve.wait_ge(sem("s1"), NK)
            dve.wait_ge(sem("nrm"), NK)
            for j in range(2):
                dve.wait_ge(sem(f"v_st{j}"), (NK + 1 - j) // 2 * 16)
            dve.memset(cmax[:], 0.0).then_inc(sem("q1w"), 1)
            dve.memset(Q2[D:P, :, :].bitcast(F32), 0.0).then_inc(sem("q20"), 1)
            dve.memset(oT_a[:], 1.0).then_inc(sem("o_cp"), 1)

            def q_stage(v, src):
                if not isinstance(v, int) or v:
                    dve.wait_ge(sem("qT_mm"), v)
                dve.tensor_copy(qst[:], qnat[:, bass.ds(QB + src * QB, QB), :]).then_inc(sem("qst"), 1)

            def q_lo(v, par):
                dve.wait_ge(sem("q2"), v + 1)
                dve.wait_ge(sem("q1h"), v + 1)
                dve.tensor_tensor(Q1[0:D, par, :], bT[0:D, 0, :], Q2[0:D, par, :].bitcast(F32), ALU.subtract)\
                    .then_inc(sem("q_lo"), 1)

            def piece(v, k):
                i, g = divmod(k, NG)
                w = min(PIECE, KEYS - g * PIECE)
                dve.wait_ge(sem("m_mm"), NM * v + k + 1)
                if w > 512:
                    src = bM[:, :, :].rearrange("p b c -> p (b c)")[:, 0:w]
                else:
                    src = bM[:, 0, 0:w]
                dve.tensor_reduce(mpart[:, i, g:g + 1], src, AX, ALU.max).then_inc(sem("m_red"), 1)

            def maxima(v):
                dve.wait_ge(sem("m_red"), NM * v + NM)
                if not isinstance(v, int) or v:
                    dve.wait_ge(sem("cT_mm"), v)
                dve.tensor_reduce(cmax[:], mpart[:], AX, ALU.max).then_inc(sem("cmax"), 1)

            def o_out(v):
                dve.wait_ge(sem("oT_a"), v + 1)
                o = bT[:, 0, 0:QB * (D + 1)].rearrange("p (i d) -> p i d", i=QB)
                dve.reciprocal(orec[:], o[:, :, D]).then_inc(sem("orec"), 1)
                dve.wait_ge(sem("orec"), v + 1)
                dve.tensor_tensor(qnat[:, bass.ds(v * QB, QB), 0:D], o[:, :, 0:D],
                                  orec[:].unsqueeze(2).to_broadcast([P, QB, D]), ALU.mult).then_inc(sem("o_ev"), 1)

            def p_lo(u, p):
                w = 2 if 2 * p + 1 < NK else 1
                dve.wait_ge(sem("p_hi"), NP * u + p + 1)
                dve.tensor_tensor(Pl[:, p % 3, 0:w, :], PT[:, p % 3, 0:w, :],
                                  Ph[:, p % 3, 0:w, :].bitcast(F32), ALU.subtract).then_inc(sem("p_lo"), 1)

            def unit(u, j, last):
                q_stage(u + 1, (u + 1) % UNITS if last else u + 1)
                for p in range(NP):
                    if (p, 0) in SLOTS:
                        piece(u + 1, SLOTS.index((p, 0)))
                    if p:
                        p_lo(u, p - 1)
                    if p == 0:
                        q_lo(u + 1, (j + 1) % 2)
                    if p == 2:
                        o_out(u)
                    if (p, 1) in SLOTS:
                        piece(u + 1, SLOTS.index((p, 1)))
                    if p == SLOTS[-1][0]:
                        maxima(u + 1)
                p_lo(u, NP - 1)

            dve.wait_ge(sem("q1w"), 1)
            q_stage(0, 0)
            q_lo(0, 0)
            for k in range(NM):
                piece(0, k)
            maxima(0)
            for h in range(H):
                with dve.Fori(0, NB // 2) as i:
                    for j in range(2):
                        unit(NB * h + 2 * i + j, j, h == H - 1 and j == 1)
            o_out(UNITS)

            dve.wait_ge(sem("wst0"), E * (EW // WC) // 2 * 32)
            dve.wait_ge(sem("wst1"), E * (EW // WC) // 2 * 32)
            dve.wait_ge(sem("o_ev"), UNITS + 1)
            dve.wait_ge(sem("c_bo"), 16)

            def fin(s, a, b, d):
                if a:
                    if not (s.i is None and s.off < 2):
                        dve.wait_ge(sem("oT_mm"), s.v - 1)
                    dve.tensor_copy(heads(ost[:, s.par, :]), q_by_head[:, :, s.v, 0:D]).then_inc(sem("ost"), 1)
                if b:
                    t = s.back(1)
                    dve.wait_ge(sem(f"xin{t.par}"), 16 * t.half + 16)
                    if not (t.i is None and t.off < 2):
                        dve.wait_ge(sem(f"ox{t.par}"), 16 * t.half)
                        dve.wait_ge(sem(f"ol{t.par}"), 16 * t.half)
                        dve.wait_ge(sem("x3T_mm"), t.v - 1)
                    dve.tensor_tensor(x2[:, t.par, :], xin[:, t.par, :], bob[:], ALU.add).then_inc(sem("xb"), 1)
                    dve.wait_ge(sem("xb"), t.v + 1)
                    dve.wait_ge(sem("y_mm"), t.v + 1)
                    dve.tensor_tensor(x2[:, t.par, :], x2[:, t.par, :], bFY[t.par][:, 0, 0:DIM], ALU.add)\
                        .then_inc(sem("x2"), 1)
                    dve.wait_ge(sem("x2"), t.v + 1)
                    dve.bn_stats(st2[:], x2[:, t.par, :]).then_inc(sem("st2"), 1)
                    dve.wait_ge(sem("st2"), t.v + 1)
                    dve.sem_inc(sem("dve_held"), 1)
                    dve.bn_aggr(mv2[:], st2[:]).then_inc(sem("mv2"), 1)
                if d:
                    q = s.back(3)
                    dve.wait_ge(sem("lg_mm"), q.v + 1)
                    dve.tensor_copy(lg[:, q.v, :], bL[:, 0, 0:E]).then_inc(sem("lg"), 1)
                if b:
                    dve.wait_ge(sem("sd2"), t.v + 1)
                    dve.reciprocal(rs2[:], sd2[:]).then_inc(sem("rs2"), 1)
                    dve.wait_ge(sem("rs2"), t.v + 1)
                    dve.wait_ge(sem("mv2"), t.v + 1)
                    dve.tensor_scalar(x3[:, t.par, :], x2[:, t.par, :], mv2[:, 0:1], rs2[:, 0:1],
                                      ALU.subtract, ALU.mult).then_inc(sem("x3"), 1)

            for lo, hi, a in ((0, 1, (1, 0, 0)), (1, 3, (1, 1, 0)), (3, NT, (1, 1, 1)), (NT, NT + 1, (0, 1, 1)),
                              (NT + 1, NT + 3, (0, 0, 1))):
                run_steps(dve, lo, hi, lambda s, a=a: fin(s, *a))

            def over_e(ap):
                return ap.unsqueeze(2).to_broadcast([P, NT, E])

            dve.wait_ge(sem("lg"), NT)
            dve.wait_ge(sem("iota"), 3)
            link(dve.tensor_copy(iot[:], iot_i[:]))
            link(dve.tensor_copy(tid[:], tid_i[:]))
            link(dve.tensor_copy(pc[:], pc_i[:]))
            link(dve.tensor_scalar(thr[:], iot[:, 0:NBLK + 1], float(P), None, ALU.mult))
            link(dve.tensor_scalar(w8[:], iot[:, 0:E], -1.0, float(E), ALU.mult, ALU.add))
            link(dve.tensor_reduce(sm[:], lg[:], AX, ALU.max))
            dve.tensor_tensor(rb[:], lg[:], over_e(sm[:]), ALU.subtract).then_inc(sem("r_sh"), 1)
            dve.wait_ge(sem("r_ex"), 1)
            link(dve.tensor_reduce(sm[:], ra[:], AX, ALU.add))
            link(dve.reciprocal(sm[:], sm[:]))
            link(dve.tensor_tensor(pr[:], ra[:], over_e(sm[:]), ALU.mult))
            w8b = w8[:].unsqueeze(1).to_broadcast([P, NT, E])
            for k in range(2):
                link(dve.tensor_reduce(top_p[:, k, :], pr[:], AX, ALU.max))
                link(dve.tensor_tensor(ra[:], pr[:], over_e(top_p[:, k, :]), ALU.is_equal))
                link(dve.tensor_tensor(ra[:], ra[:], w8b, ALU.mult))
                link(dve.tensor_reduce(sm[:], ra[:], AX, ALU.max))
                link(dve.tensor_tensor(oh[:, k, :, :], w8b, over_e(sm[:]), ALU.is_equal))
                if k == 0:
                    link(dve.scalar_tensor_tensor(pr[:], oh[:, 0, :, :], -2.0, pr[:], ALU.mult, ALU.add))
            dve.tensor_tensor(M[:], oh[:, 0, :, :], oh[:, 1, :, :], ALU.add).then_inc(sem("M"), 1)
            link(dve.tensor_tensor(sm[:], top_p[:, 0, :], top_p[:, 1, :], ALU.add))
            link(dve.tensor_scalar(sm[:], sm[:], 1e-6, None, ALU.add))
            link(dve.reciprocal(sm[:], sm[:]))
            link(dve.tensor_tensor(wgt[:], top_p[:], sm[:].unsqueeze(1).to_broadcast([P, 2, NT]), ALU.mult))

            dve.wait_ge(sem("tot_mm"), 1)
            link(dve.tensor_copy(tot[:], bR[:, 0, P:2 * P].rearrange("p (t e) -> p t e", e=E)))
            link(dve.tensor_copy(ra[:], tot[:]))
            a_, b_ = ra, rb
            k = 1
            while k < NT:
                link(dve.tensor_copy(b_[:, 0:k, :], a_[:, 0:k, :]))
                link(dve.tensor_tensor(b_[:, k:NT, :], a_[:, k:NT, :], a_[:, 0:NT - k, :], ALU.add))
                a_, b_ = b_, a_
                k *= 2
            cnt = nb
            link(dve.tensor_copy(cs[:, 0, :], a_[:, NT - 1, :]))
            link(dve.tensor_tensor(cmp8[:], cs[:, 0, :].unsqueeze(2).to_broadcast([P, E, NT]),
                                   thr[:, 0:NT].unsqueeze(1).to_broadcast([P, E, NT]), ALU.is_gt))
            link(dve.tensor_reduce(nb[:], cmp8[:], AX, ALU.add))
            link(dve.tensor_copy(cs[:, 0, :], nb[:]))
            c = 0
            k = 1
            while k < E:
                link(dve.tensor_copy(cs[:, 1 - c, 0:k], cs[:, c, 0:k]))
                link(dve.tensor_tensor(cs[:, 1 - c, k:E], cs[:, c, k:E], cs[:, c, 0:E - k], ALU.add))
                c = 1 - c
                k *= 2
            link(dve.tensor_tensor(st128[:], cs[:, c, :], nb[:], ALU.subtract))
            link(dve.tensor_scalar(st128[:], st128[:], float(P), None, ALU.mult))
            link(dve.tensor_tensor(a_[:], a_[:], tot[:], ALU.subtract))
            link(dve.tensor_tensor(a_[:], a_[:], st128[:].unsqueeze(1).to_broadcast([P, NT, E]), ALU.add))
            link(dve.tensor_tensor(a_[:], a_[:], bR[:, 0, 0:P].rearrange("p (t e) -> p t e", e=E), ALU.add))
            for k in range(2):
                link(dve.tensor_tensor(b_[:], oh[:, k, :, :], a_[:], ALU.mult))
                link(dve.tensor_reduce(pos[:, k, :], b_[:], AX, ALU.add))
            link(dve.tensor_tensor(ecmp[:], iot[:, 0:NBLK].unsqueeze(2).to_broadcast([P, NBLK, E - 1]),
                                   cs[:, c, 0:E - 1].unsqueeze(1).to_broadcast([P, NBLK, E - 1]), ALU.is_ge))
            link(dve.tensor_reduce(ef[:], ecmp[:], AX, ALU.add))
            link(dve.tensor_copy(zt[:], ef[:]))
            w = NBLK - 1
            link(dve.scalar_tensor_tensor(zt[:, 0:w], ef[:, 1:NBLK], float(E), ef[:, 0:w], ALU.mult, ALU.add))
            w = NBLK - 2
            link(dve.scalar_tensor_tensor(zt[:, 0:w], ef[:, 2:NBLK], float(E * E), zt[:, 0:w], ALU.mult, ALU.add))
            link(dve.tensor_copy(eid[:], zt[:]))
            flat = pos[:].rearrange("p k t -> p (k t)")
            R = 2 * NT
            link(dve.tensor_tensor(G[:], flat.unsqueeze(2).to_broadcast([P, R, NBLK + 1]),
                                   thr[:].unsqueeze(1).to_broadcast([P, R, NBLK + 1]), ALU.is_ge))
            link(dve.tensor_reduce(rr[:].rearrange("p k t -> p (k t)"), G[:], AX, ALU.add))
            link(dve.scalar_tensor_tensor(rr[:], rr[:], -float(P), pos[:], ALU.mult, ALU.add))
            link(dve.tensor_scalar(rr[:], rr[:], float(P), None, ALU.add))
            link(dve.tensor_tensor(ohr[:], iot[:].unsqueeze(1).to_broadcast([P, R, P]),
                                   rr[:].rearrange("p k t -> p (k t)").unsqueeze(2).to_broadcast([P, R, P]),
                                   ALU.is_equal))
            link(dve.tensor_tensor(mov[:, :, 1, :], G[:, :, 0:NBLK], G[:, :, 1:NBLK + 1], ALU.subtract))
            for k in range(2):
                link(dve.tensor_tensor(mov[:, k * NT:(k + 1) * NT, 0, :], mov[:, k * NT:(k + 1) * NT, 1, :],
                                       tid[:].unsqueeze(2).to_broadcast([P, NT, NBLK]), ALU.mult))
            dve.tensor_tensor(mov[:, :, 1, :], mov[:, :, 1, :],
                              wgt[:].rearrange("p k t -> p (k t)").unsqueeze(2).to_broadcast([P, R, NBLK]),
                              ALU.mult).then_inc(sem("mov"), 1)
            dve.wait_ge(sem("tab_mm"), 1)
            link(dve.tensor_copy(tok[:], bR[:, 0, 256:256 + NBLK]))
            link(dve.tensor_copy(wtab[:], bR[:, 0, 256 + NBLK:256 + 2 * NBLK]))
            link(dve.tensor_scalar(gidx[:], tok[:], -1.0, 0.0, ALU.add, ALU.max))
            link(dve.tensor_scalar(zt[:], tok[:], 0.0, pc[:, 0:1], ALU.is_equal, ALU.mult))
            dve.scalar_tensor_tensor(sidx[:], tok[:], -1.0, zt[:], ALU.add, ALU.add).then_inc(sem("routed"), 1)

            def ffn(s, x_, g, h):
                if h:
                    t = s.back(2)
                    dve.wait_ge(sem("hhi"), t.v + 1)
                    dve.tensor_tensor(hTe[:, 1, :, :], bH[:, 0, :].rearrange("p (k c) -> p k c", k=I // P),
                                      hTe[:, 0, :, :].bitcast(F32), ALU.subtract).then_inc(sem("hlo"), 1)
                if g:
                    t = s.back(1)
                    dve.wait_ge(sem("silu"), t.v + 1)
                    dve.wait_ge(sem("u_mm"), t.v + 1)
                    dve.tensor_tensor(hs[:], hs[:], bU[t.par][:, 0, :], ALU.mult).then_inc(sem("hs"), 1)
                if x_:
                    dve.wait_ge(sem("xhi"), s.v + 1)
                    dve.tensor_tensor(xTe[:, s.par, 1, :, :],
                                      bXe[:, 0, 0:DIM].rearrange("p (k c) -> p k c", k=2),
                                      xTe[:, s.par, 0, :, :].bitcast(F32), ALU.subtract).then_inc(sem("xlo"), 1)
                if h:
                    t = s.back(2)
                    dve.wait_ge(sem("y_e"), t.v + 1)
                    if not (t.i is None and t.off < 2):
                        dve.wait_ge(sem(f"add{t.par}"), 16 * t.half)
                    dve.tensor_scalar(ysb[:, t.par, :], bY[:, 0, 0:DIM], wtab[:, bass.ds(t.v, 1)], None, ALU.mult)\
                        .then_inc(sem("ysb"), 1)

            for lo, hi, a in FFN_SEGMENTS:
                run_steps(dve, lo, hi, lambda s, a=a: ffn(s, *a))

        @block.tensor
        def _(pe):
            pe.wait_ge(sem("ident"), 1)

            def pro(s, c, a, b):
                if c:
                    t = s.back(3)
                    pe.wait_ge(sem("knat"), t.v + 1)
                    pe.wait_ge(sem("kmask"), t.v + 1)
                    if not (t.i is None and t.off < 1):
                        pe.wait_ge(sem("s2"), t.v)
                        pe.wait_ge(sem("klo"), t.v)
                    for h in range(H):
                        last = pe.transpose(bK[0:A, 0, h * P:(h + 1) * P], knat[:, t.par, h, :], ident[:])
                    last.then_inc(sem("kT_mm"), 1)
                if a:
                    pe.wait_ge(sem("ln"), s.v + 1)
                    for k in range(2):
                        r = P if (k == 0 or a == 'l') else CIN - P
                        last = pe.transpose(bX[s.par][0:r, 0, k * P:(k + 1) * P],
                                            xn[:, s.par, k * P:k * P + r], ident[:])
                    last.then_inc(sem("xT_mm"), 1)
                if b:
                    t = s.back(1)
                    pe.wait_ge(sem("xT"), 2 * t.v + 2)
                    if not (t.i is None and t.off < 2):
                        pe.wait_ge(sem("v_lo"), t.v - 1)
                        pe.wait_ge(sem("knat"), t.v - 1)
                    w, lo = (wl, 0) if b == 'l' else (wc, DIM)
                    n = 2 * DIM - lo
                    for k in range(2):
                        last = pe.matmul(bA[t.par][:, 0, lo:2 * DIM], xT[:, t.par, k, :], w[:, k, 0:n],
                                         start=k == 0, stop=k == 1)
                    last.then_inc(sem("qk_mm"), 1)
                    for k in range(2):
                        last = pe.matmul(bV[t.par][:, 0, 0:DIM], xT[:, t.par, k, :], w[:, k, n:n + DIM],
                                         start=k == 0, stop=k == 1)
                    last.then_inc(sem("v_mm"), 1)

            pe.wait_ge(sem("kn0"), 1)
            run_steps(pe, 0, 1, lambda s: pro(s, 0, 'c', 0))
            pe.wait_ge(sem("wc_in"), 16)
            pe.wait_ge(sem("wc_in2"), 16)
            pe.wait_ge(sem("wc0"), 1)
            run_steps(pe, 1, 3, lambda s: pro(s, 0, 'c', 'c'))
            run_steps(pe, 3, NC, lambda s: pro(s, 1, 'c', 'c'))
            pe.wait_ge(sem("wl_in"), 16)
            for lo, hi, a in ((NC, NC + 1, (1, 'l', 'c')), (NC + 1, NK, (1, 'l', 'l')),
                              (NK, NK + 1, (1, 0, 'l')), (NK + 1, NK + 3, (1, 0, 0))):
                run_steps(pe, lo, hi, lambda s, a=a: pro(s, *a))

            pe.sem_inc(sem("pv"), 3)

            def q_T(v):
                pe.wait_ge(sem("qst"), v + 1)
                if not isinstance(v, int) or v:
                    pe.wait_ge(sem("c_row"), v)
                for i in range(QB):
                    last = pe.transpose(bT[0:A, 0, i * P:(i + 1) * P], qst[:, i, :], ident[:])
                last.then_inc(sem("qT_mm"), 1)

            def piece(v, h, par, k):
                i, g = divmod(k, NG)
                if k == 0:
                    pe.wait_ge(sem("q2"), v + 1)
                if not (isinstance(v, int) and v == 0 and k == 0):
                    pe.wait_ge(sem("m_red"), NM * v + k)
                lo, hi = g * PIECE, min((g + 1) * PIECE, KEYS)
                for b, c in enumerate(range(lo, hi, 512)):
                    w = min(512, hi - c)
                    last = pe.matmul(bM[:, b, 0:w], Q2[:, par, i * P:(i + 1) * P], S2[:, h, c:c + w],
                                     start=True, stop=True)
                last.then_inc(sem("m_mm"), 1)

            def c_T(v):
                pe.wait_ge(sem("cmax"), v + 1)
                if isinstance(v, int) and v == 0:
                    pe.wait_ge(sem("q1h"), 1)
                    pe.wait_ge(sem("q_lo"), 1)
                else:
                    pe.wait_ge(sem("o_ev"), v)
                for i in range(QB):
                    last = pe.transpose(bT[0:1, 0, i * P:(i + 1) * P], cmax[:, i:i + 1], ident[:])
                last.then_inc(sem("cT_mm"), 1)

            def o_T(v):
                pe.wait_ge(sem("o_cp"), v + 1)
                if not isinstance(v, int):
                    pe.wait_ge(sem("q1h"), v + 2)
                    pe.wait_ge(sem("q_lo"), v + 2)
                else:
                    pe.wait_ge(sem("c_row"), v + 1)
                for i in range(QB):
                    last = pe.transpose(bT[:, 0, i * (D + 1):(i + 1) * (D + 1)], oT_a[0:D + 1, i * P:(i + 1) * P],
                                        ident[0:D + 1, 0:D + 1])
                last.then_inc(sem("oT_a"), 1)

            pe.wait_ge(sem("klo"), NK)
            pe.wait_ge(sem("s1"), NK)
            pe.wait_ge(sem("v_lo"), NK)
            pe.wait_ge(sem("q20"), 1)
            q_T(0)
            for k in range(NM):
                piece(0, 0, 0, k)
            c_T(0)

            def unit(h, u, j, hn):
                def scores(p):
                    g = NP * u + p
                    sl = (NP * j + p) % 2
                    if p == 0:
                        pe.wait_ge(sem("c_row"), u + 1)
                    pe.wait_ge(sem("exp"), g + 1)
                    for b, c in enumerate(range(2 * p, min(2 * p + 2, NK))):
                        pe.matmul(bS[sl][:, b, :], S1[:, h, c * P:(c + 1) * P], Q1[:, j, :], start=True, stop=False)
                        last = pe.matmul(bS[sl][:, b, :], S2[:, h, c * P:(c + 1) * P], Q2[:, j, :],
                                         start=False, stop=True)
                    last.then_inc(sem("s_mm"), 1)

                def outputs(p):
                    g = NP * u + p
                    sl = p % 3
                    if p == 0:
                        pe.wait_ge(sem("o_cp"), u + 1)
                    tiles = list(enumerate(range(2 * p, min(2 * p + 2, NK))))
                    pe.wait_ge(sem("p_hi"), g + 1)
                    for b, c in tiles:
                        pe.matmul(bPV[0:D + 1, 0, :], V[:, h % 2, c, 0:D + 1], Ph[:, sl, b, :],
                                  start=c == 0, stop=False, skip_group_check=True)
                        pe.matmul(bPV[0:D, 0, :], V[:, h % 2, c, D + 1:VW], Ph[:, sl, b, :],
                                  start=False, stop=False, skip_group_check=True)
                    pe.wait_ge(sem("p_lo"), g + 1)
                    for b, c in tiles:
                        last = pe.matmul(bPV[0:D + 1, 0, :], V[:, h % 2, c, 0:D + 1],
                                         Pl[:, sl, b, :],
                                         start=False, stop=c == NK - 1, skip_group_check=True)
                    last.then_inc(sem("pv"), 1)

                for p in range(NP):
                    scores(p)
                    if p == 0:
                        q_T(u + 1)
                    if (p, 0) in SLOTS:
                        piece(u + 1, hn, (j + 1) % 2, SLOTS.index((p, 0)))
                    if p == 2:
                        o_T(u)
                    if p >= 2:
                        outputs(p - 2)
                    if (p, 1) in SLOTS:
                        piece(u + 1, hn, (j + 1) % 2, SLOTS.index((p, 1)))
                c_T(u + 1)
                outputs(NP - 2)
                outputs(NP - 1)

            for h in range(H):
                pe.wait_ge(sem(f"v_in{h % 2}"), 16 * (h // 2) + 16)
                with pe.Fori(0, NB // 2) as i:
                    for j in range(2):
                        hn = h if j == 0 else (h + (i + 1) // (NB // 2)) % H
                        unit(h, NB * h + 2 * i + j, j, hn)
            o_T(UNITS)

            pe.wait_ge(sem("c_wo"), 16)
            pe.wait_ge(sem("c_rt"), 16)

            def fin(s, a, b, c, d):
                if a:
                    pe.wait_ge(sem("ost"), s.v + 1)
                    for k in range(2):
                        last = pe.transpose(bFT[s.par][:, 0, k * P:(k + 1) * P], ost[:, s.par, k * P:(k + 1) * P],
                                            ident[:])
                    last.then_inc(sem("oT_mm"), 1)
                if b:
                    t = s.back(1)
                    pe.wait_ge(sem("oT"), t.v + 1)
                    if not (t.i is None and t.off < 2):
                        pe.wait_ge(sem("x2"), t.v - 1)
                    for k in range(2):
                        last = pe.matmul(bFY[t.par][:, 0, 0:DIM], oT[:, t.par, k, :], wot[:, k, :],
                                         start=k == 0, stop=k == 1)
                    last.then_inc(sem("y_mm"), 1)
                if d:
                    t = s.back(3)
                    pe.wait_ge(sem("x3T"), t.v + 1)
                    if not (t.i is None and t.off < 1):
                        pe.wait_ge(sem("lg"), t.v)
                    for k in range(2):
                        last = pe.matmul(bL[:, 0, 0:E], x3T[:, t.par, k, :], rt[:, k, :],
                                         start=k == 0, stop=k == 1)
                    last.then_inc(sem("lg_mm"), 1)
                if c:
                    t = s.back(2)
                    pe.wait_ge(sem("x3"), t.v + 1)
                    for k in range(2):
                        last = pe.transpose(bFX[t.par][:, 0, k * P:(k + 1) * P], x3[:, t.par, k * P:(k + 1) * P],
                                            ident[:])
                    last.then_inc(sem("x3T_mm"), 1)

            for lo, hi, a in ((0, 1, (1, 0, 0, 0)), (1, 2, (1, 1, 0, 0)), (2, 3, (1, 1, 1, 0)), (3, NT, (1, 1, 1, 1)),
                              (NT, NT + 1, (0, 1, 1, 1)), (NT + 1, NT + 2, (0, 0, 1, 1)), (NT + 2, NT + 3, (0, 0, 0, 1))):
                run_steps(pe, lo, hi, lambda s, a=a: fin(s, *a))

            pe.wait_ge(sem("M"), 1)
            pe.wait_ge(sem("U"), 1)
            pe.wait_ge(sem("ones"), 1)
            Mf = M[:].rearrange("p t e -> p (t e)")
            pe.matmul(bR[:, 0, 0:P], U[:], Mf, start=True, stop=True)
            pe.matmul(bR[:, 0, P:2 * P], ones[:], Mf, start=False, stop=True, skip_group_check=True)\
                .then_inc(sem("tot_mm"), 1)
            pe.wait_ge(sem("mov"), 1)
            for k in range(2 * NT):
                last = pe.matmul(bR[:, 0, 256:256 + 2 * NBLK], ohr[:, k, :], mov[:, k, :, :].rearrange("p a b -> p (a b)"),
                                 start=k == 0, stop=k == 2 * NT - 1)
            last.then_inc(sem("tab_mm"), 1)

            pe.wait_ge(sem("routed"), 1)

            def three(out_ap, st_hi, st_lo, w, e, lo, n, first, last_):
                pe.matmul(out_ap, st_hi, w[:, e, 0, lo:lo + n], start=first, stop=False)
                pe.matmul(out_ap, st_lo, w[:, e, 0, lo:lo + n], start=False, stop=False)
                return pe.matmul(out_ap, st_hi, w[:, e, 1, lo:lo + n], start=False, stop=last_)

            def experts(b):
                v = pe.value_load(eid[0:1, bass.ds(b, 1)], min_val=0, max_val=E ** 3 - 1)
                return v % E, v // E % E, v // (E * E)

            def ffn(s, x_, g, h, eg, eh):
                if h:
                    tb = s.back(2)
                    pe.wait_ge(sem("hs"), tb.v + 1)
                    if not (tb.i is None and tb.off < 1):
                        pe.wait_ge(sem("hlo"), tb.v)
                    for k in range(I // P):
                        last = pe.transpose(bH[:, 0, k * P:(k + 1) * P], hs[:, k * P:(k + 1) * P], ident[:])
                    last.then_inc(sem("hT_mm"), 1)
                if g:
                    t = s.back(1)
                    pe.wait_ge(sem("w_in"), eg + 1)
                    pe.wait_ge(sem("xlo"), t.v + 1)
                    if not (t.i is None and t.off < 2):
                        pe.wait_ge(sem("hs"), t.v - 1)
                    for k in range(2):
                        last = three(bG[t.par][:, 0, :], xTe[:, t.par, 0, k, :], xTe[:, t.par, 1, k, :], W, eg,
                                     k * 2 * I, I, k == 0, k == 1)
                    last.then_inc(sem("g_mm"), 1)
                    for k in range(2):
                        last = three(bU[t.par][:, 0, :], xTe[:, t.par, 0, k, :], xTe[:, t.par, 1, k, :], W, eg,
                                     k * 2 * I + I, I, k == 0, k == 1)
                    last.then_inc(sem("u_mm"), 1)
                if x_:
                    pe.wait_ge(sem(f"g_in{s.par}"), 16 * s.half + 16)
                    if not (s.i is None and s.off < 1):
                        pe.wait_ge(sem("xlo"), s.v)
                    for k in range(2):
                        last = pe.transpose(bXe[:, 0, k * P:(k + 1) * P], xg[:, s.par, k * P:(k + 1) * P], ident[:])
                    last.then_inc(sem("xTe_mm"), 1)
                if h:
                    pe.wait_ge(sem("hlo"), tb.v + 1)
                    if not (tb.i is None and tb.off < 1):
                        pe.wait_ge(sem("ysb"), tb.v)
                    for k in range(I // P):
                        last = three(bY[:, 0, 0:DIM], hTe[:, 0, k, :], hTe[:, 1, k, :], W, eh,
                                     2 * 2 * I + k * DIM, DIM, k == 0, k == I // P - 1)
                    last.then_inc(sem("y_e"), 1)

            ffn(Step(None, 0), 1, 0, 0, None, None)
            e0, e1, _ = experts(0)
            ffn(Step(None, 1), 1, 1, 0, e0, None)
            ffn(Step(None, 2), 1, 1, 1, e1, e0)
            e1, e2, e3 = experts(1)
            ffn(Step(None, 3), 1, 1, 1, e2, e1)
            ffn(Step(None, 4), 1, 1, 1, e3, e2)
            with pe.Fori(0, (NBLK - 5) // 2) as i:
                eh, eg, en = experts(2 * i + 3)
                ffn(Step(i, 5), 1, 1, 1, eg, eh)
                ffn(Step(i, 6), 1, 1, 1, en, eg)
            eh, eg, _ = experts(NBLK - 2)
            ffn(Step(None, NBLK), 0, 1, 1, eg, eh)
            ffn(Step(None, NBLK + 1), 0, 0, 1, None, eg)


UNITS = H * NB
CTX_LOADS = ((0, 2), (2, NC - 1))
LAT_AT = 6
SLOTS = sorted([(p, 0) for p in range(1, NP - 1)] + [(p, 1) for p in (4, 7, 10)])
assert len(SLOTS) == NM

FFN_SEGMENTS = ((0, 1, (1, 0, 0)), (1, 2, (1, 1, 0)), (2, NBLK, (1, 1, 1)), (NBLK, NBLK + 1, (0, 1, 1)),
                (NBLK + 1, NBLK + 2, (0, 0, 1)))


def kernel(**inputs):
    import numpy as np
    import concourse.bacc as bacc
    from concourse.bass_utils import run_bass_kernel_spmd as run

    a = {k.replace("L0_xattn_", "").replace("L0_ffn_", ""): np.asarray(v) for k, v in inputs.items()}
    arrays = {
        "x": a["x"][0], "ctx_in": a["ctx_768"][0], "mask": a["mask_BxS2_bk0"][0],
        "ln_x_g": a["ln_x_g"], "ln_x_b": a["ln_x_b"], "ln_l_g": a["ln_l_g"], "ln_l_b": a["ln_l_b"],
        "qn_g": a["qn_g"], "kn_g": a["kn_g"],
        "w_lat": np.concatenate([a["Wq"], a["Wlkv"]], axis=0).T, "w_ctx": a["Wkv"].T,
        "wo_t": a["Wo"].T, "bo": a["bo"], "router_t": a["router_w"].T, "w13": a["w13"], "w2": a["w2"],
    }
    nc = bacc.Bacc("TRN2", target_bir_lowering=False, num_devices=1)
    args = {}
    for name in arrays:
        arrays[name] = np.ascontiguousarray(arrays[name])
        args[name] = nc.dram_tensor(name, arrays[name].shape, mybir.dt.from_np(arrays[name].dtype),
                                    kind="ExternalInput").ap()
    args["out"] = nc.dram_tensor("out", [TOK + BLK, DIM], F32, kind="ExternalOutput").ap()
    build(nc, **args)
    r = run(nc, [arrays], core_ids=[0])
    return np.asarray(r.results[0]["out"])[0:TOK].reshape(1, TOK, DIM)
```

```python
import concourse.bass as bass
from concourse import mybir
from contextlib import ExitStack

F32 = mybir.dt.float32
F32R = mybir.dt.float32r
I32 = mybir.dt.int32
U8 = mybir.dt.uint8
ALU = mybir.AluOpType
ACT = mybir.ActivationFunctionType
AX = mybir.AxisListType.X

P = 128
TOK, DIM = 2048, 256
CTX, CIN = 1601, 192
H, D = 4, 64
E, I = 8, 512
NT = TOK // P
NC = -(-CTX // P)
NK = NC + NT
KEYS = NK * P
A = D + 2
QB = 4
NB = NT // QB
VW = 2 * D + 1
NP = (NK + 1) // 2
NG = -(-KEYS // 512)
PIECE = KEYS // NG
assert PIECE * NG == KEYS
NM = QB * NG
ROWS = 2 * TOK
BLK = P
NBLK = (ROWS - E) // BLK + E
EW = (DIM // P) * 2 * I + (I // P) * DIM
WC = 256
BIG = 1e30
SCALE = D ** -0.5
LN_EPS = 1e-5
RMS_EPS = 1e-8


class Step:

    def __init__(self, i, off):
        self.i, self.off = i, off

    @property
    def v(self):
        return self.off if self.i is None else 2 * self.i + self.off

    @property
    def half(self):
        return self.off // 2 if self.i is None else self.i + self.off // 2

    @property
    def par(self):
        return self.off % 2

    def back(self, k):
        return Step(self.i, self.off - k)


def run_steps(eng, lo, hi, body):
    if (hi - lo) % 2 or hi - lo < 4 or lo < 5:
        body(Step(None, lo))
        if hi - lo > 1:
            run_steps(eng, lo + 1, hi, body)
        return
    with eng.Fori(0, (hi - lo) // 2) as i:
        body(Step(i, lo))
        body(Step(i, lo + 1))


def build(nc, x, ctx_in, mask, ln_x_g, ln_x_b, ln_l_g, ln_l_b, qn_g, kn_g, w_lat, w_ctx, wo_t, bo,
          router_t, w13, w2, out):
    xln_d = nc.dram_tensor("xln_d", [TOK, DIM], F32, kind="Internal").ap()
    v_d = nc.dram_tensor("v_d", [H, P, NK, VW], F32, kind="Internal").ap()
    wsp_d = nc.dram_tensor("wsp_d", [4 * E, P, EW // 2], F32, kind="Internal").ap()
    stack = ExitStack()

    def sb(name, shape, dt=F32, at=stack):
        return at.enter_context(nc.sbuf_tensor(name, shape, dt))

    def bank(name, n=1, at=stack):
        return at.enter_context(nc.psum_tensor(name, [P, n, 512], F32))

    with stack:
        names = {}

        def sem(name):
            if name not in names:
                names[name] = stack.enter_context(nc.semaphore(name))
            return names[name]

        ident = sb("ident", [P, P])
        wtab = sb("wtab", [P, NBLK])
        gidx = sb("gidx", [P, NBLK], I32)
        sidx = sb("sidx", [P, NBLK], I32)
        eid = sb("eid", [P, NBLK], I32)
        ring_g = sb("ring_g", [P, 2], I32)
        ring_s = sb("ring_s", [P, 2], I32)
        mcol = sb("mcol", [P, NK])
        cols = sb("cols", [P, 8])
        eps = sb("eps", [P, 1])
        pro = ExitStack()
        ctxt = sb("ctxt", [P, NC, CIN], at=pro)
        knat = sb("knat", [P, 2, H, A], at=pro)
        xn = sb("xn", [P, 2, DIM], at=pro)
        pro.close()
        Ph = sb("Ph", [P, 3, 2, QB * P], F32R, at=pro)
        pro.close()
        xg = sb("xg", [P, 2, DIM])
        xTe = sb("xTe", [P, 2, 2, 2, P], F32R)
        hs = sb("hs", [P, I])
        hTe = sb("hTe", [P, 2, I // P, P], F32R)
        ysb = sb("ysb", [P, 2, DIM])

        big = ExitStack()
        S1 = sb("S1", [P, H, KEYS], F32R, at=big)
        S2 = sb("S2", [P, H, KEYS], F32R, at=big)
        qnat = sb("qnat", [P, QB + H * NT, A], at=big)
        top = ExitStack()
        t0 = ExitStack()
        xall = sb("xall", [P, NT, DIM], at=t0)
        wl = sb("wl", [P, 2, 3 * DIM], at=t0)
        wc = sb("wc", [P, 2, 2 * DIM], at=t0)
        xT = sb("xT", [P, 2, 2, P], at=t0)
        m_u8 = sb("m_u8", [P, NC], U8, at=t0)
        gq = sb("gq", [P, 2, D], at=t0)
        gs = sb("gs", [P, D], at=t0)
        mvs = sb("mvs", [P, NK, 2], at=t0)
        st6 = sb("st6", [P, NK, 6], at=t0)
        rsd = sb("rsd", [P, NK], at=t0)
        sda = sb("sda", [P, NK], at=t0)
        va = sb("va", [P, NK], at=t0)
        ss = sb("ss", [P, 2 * H], at=t0)
        nrm = sb("nrm", [P, 2 * H], at=t0)
        rn0 = sb("rn0", [P, 2 * H], at=t0)
        rn = sb("rn", [P, 2 * H], at=t0)
        Vs = sb("Vs", [P, 2, H, VW], F32R, at=t0)
        t0.close()
        t1 = ExitStack()
        V = sb("V", [P, 2, NK, VW], F32R, at=t1)
        Q1 = sb("Q1", [P, 2, QB * P], F32R, at=t1)
        Q2 = sb("Q2", [P, 2, QB * P], F32R, at=t1)
        part = ExitStack()
        PT = sb("PT", [P, 3, 2, QB * P], at=part)
        part.close()
        Pl = sb("Pl", [P, 3, 2, QB * P], F32R, at=t1)
        qst = sb("qst", [P, QB, A], at=t1)
        wraw = sb("wraw", [P, 2, WC], at=t1)
        whi = sb("whi", [P, 2, WC], F32R, at=t1)
        oT_a = sb("oT_a", [P, QB * P], at=t1)
        mpart = sb("mpart", [P, QB, NG], at=t1)
        cmax = sb("cmax", [P, QB], at=t1)
        orec = sb("orec", [P, QB], at=t1)
        t1.close()
        top.close()
        t2 = ExitStack()
        wot = sb("wot", [P, 2, DIM], at=t2)
        rt = sb("rt", [P, 2, E], at=t2)
        bob = sb("bob", [P, DIM], at=t2)
        ost = sb("ost", [P, 2, DIM], at=t2)
        oT = sb("oT", [P, 2, 2, P], at=t2)
        xin = sb("xin", [P, 2, DIM], at=t2)
        x2 = sb("x2", [P, 2, DIM], at=t2)
        x3 = sb("x3", [P, 2, DIM], at=t2)
        x3T = sb("x3T", [P, 2, 2, P], at=t2)
        st2 = sb("st2", [P, 6], at=t2)
        mv2 = sb("mv2", [P, 2, 2], at=t2)
        sd2 = sb("sd2", [P, 2], at=t2)
        rs2 = sb("rs2", [P, 1], at=t2)
        lg = sb("lg", [P, NT, E], at=t2)
        zrow = sb("zrow", [P, DIM], at=t2)
        iot_i = sb("iot_i", [P, P], I32, at=t2)
        iot = sb("iot", [P, P], at=t2)
        tid_i = sb("tid_i", [P, NT], I32, at=t2)
        tid = sb("tid", [P, NT], at=t2)
        pc_i = sb("pc_i", [P, 1], I32, at=t2)
        pc = sb("pc", [P, 1], at=t2)
        U = sb("U", [P, P], at=t2)
        ones = sb("ones", [P, P], at=t2)
        thr = sb("thr", [P, NBLK + 1], at=t2)
        w8 = sb("w8", [P, E], at=t2)
        ra = sb("ra", [P, NT, E], at=t2)
        rb = sb("rb", [P, NT, E], at=t2)
        pr = sb("pr", [P, NT, E], at=t2)
        oh = sb("oh", [P, 2, NT, E], at=t2)
        M = sb("M", [P, NT, E], at=t2)
        tot = sb("tot", [P, NT, E], at=t2)
        top_p = sb("top_p", [P, 2, NT], at=t2)
        sm = sb("sm", [P, NT], at=t2)
        wgt = sb("wgt", [P, 2, NT], at=t2)
        pos = sb("pos", [P, 2, NT], at=t2)
        rr = sb("rr", [P, 2, NT], at=t2)
        cmp8 = sb("cmp8", [P, E, NT], at=t2)
        nb = sb("nb", [P, E], at=t2)
        cs = sb("cs", [P, 2, E], at=t2)
        st128 = sb("st128", [P, E], at=t2)
        G = sb("G", [P, 2 * NT, NBLK + 1], at=t2)
        mov = sb("mov", [P, 2 * NT, 2, NBLK], at=t2)
        ohr = sb("ohr", [P, 2 * NT, P], at=t2)
        ecmp = sb("ecmp", [P, NBLK, E - 1], at=t2)
        ef = sb("ef", [P, NBLK], at=t2)
        tok = sb("tok", [P, NBLK], at=t2)
        zt = sb("zt", [P, NBLK], at=t2)
        t2.close()
        big.close()
        W = sb("W", [P, E, 2, EW], F32R)

        ph = ExitStack()
        bX = [bank(f"bX{i}", at=ph) for i in range(2)]
        bA = [bank(f"bA{i}", at=ph) for i in range(2)]
        bV = [bank(f"bV{i}", at=ph) for i in range(2)]
        bK = bank("bK", at=ph)
        bSq = bank("bSq", at=ph)
        ph.close()
        bS = [bank(f"bS{i}", 2, at=ph) for i in range(2)]
        bM = bank("bM", 2, at=ph)
        bPV = bank("bPV", at=ph)
        bT = bank("bT", at=ph)
        ph.close()
        bFT = [bank(f"bFT{i}", at=ph) for i in range(2)]
        bFY = [bank(f"bFY{i}", at=ph) for i in range(2)]
        bFX = [bank(f"bFX{i}", at=ph) for i in range(2)]
        bL = bank("bL", at=ph)
        bR = bank("bR", at=ph)
        ph.close()
        bG = [bank(f"bG{i}", at=ph) for i in range(2)]
        bU = [bank(f"bU{i}", at=ph) for i in range(2)]
        bXe = bank("bXe", at=ph)
        bH = bank("bH", at=ph)
        bY = bank("bY", at=ph)
        ph.close()

        M_BANKS = [bM[:, i, :] for i in range(2)]
        FIRST_BANKS = M_BANKS + [bS[i][:, k, :] for i in range(2) for k in range(2)]

        block = stack.enter_context(nc.Block())

        q_by_head = qnat[:, QB:, :].rearrange("p (h t) a -> p h t a", t=NT)

        def heads(ap, lo=0, n=D):
            return ap.rearrange("p (h d) -> p h d", h=ap.shape[1] // n)

        @block.sync
        def _(sp):
            for n, (lo, hi) in enumerate(CTX_LOADS):
                sp.dma_start(ctxt[:, lo:hi, :], ctx_in[lo * P:hi * P, :].rearrange("(t p) d -> p t d", p=P))\
                    .then_inc(sem(f"ctx_in{n}"), 16)
            sp.wait_ge(sem("ctx_pad"), 1)
            sp.dma_start(ctxt[0:CTX - (NC - 1) * P, NC - 1, :], ctx_in[(NC - 1) * P:CTX, :])\
                .then_inc(sem("ctx_in_l"), 16)
            sp.dma_start(xall[:], x.rearrange("(t p) d -> p t d", p=P)).then_inc(sem("x_in"), 16)
            sp.dma_start(wl[:], w_lat.rearrange("(k p) n -> p k n", p=P)).then_inc(sem("wl_in"), 16)

            def v_store(s):
                sp.wait_ge(sem("v_lo"), s.v + 1)
                sp.dma_start(v_d[:, :, s.v, :].rearrange("h p c -> p h c"), Vs[:, s.par, :, :].bitcast(F32))\
                    .then_inc(sem(f"v_st{s.par}"), 16)

            run_steps(sp, 0, NK, v_store)

            def v_load(h):
                sp.dma_start(V[:, h % 2, :, :].bitcast(F32), v_d[h]).then_inc(sem(f"v_in{h % 2}"), 16)

            for j in range(2):
                sp.wait_ge(sem(f"v_st{j}"), (NK + 1 - j) // 2 * 16)
            sp.wait_ge(sem("klo"), NK)
            sp.wait_ge(sem("s1"), NK)
            sp.wait_ge(sem("q_s"), NT)
            v_load(0)
            v_load(1)
            NCH = EW // WC

            def src(e, ch):
                n13 = (DIM // P) * 2 * I // WC
                if ch < n13:
                    k, c = divmod(ch * WC, 2 * I)
                    return w13[e, k * P:(k + 1) * P, c:c + WC]
                k = (ch - n13) * WC // DIM
                return w2[e, k * P:(k + WC // DIM) * P, :].rearrange("(k p) n -> p k n", p=P)

            def load(e, ch):
                dst = wraw[:, ch % 2, :]
                if ch * WC >= (DIM // P) * 2 * I:
                    dst = dst.rearrange("p (k n) -> p k n", n=DIM)
                sp.dma_start(dst, src(e, ch)).then_inc(sem(f"raw{ch % 2}"), 16)

            load(0, 0)
            load(0, 1)
            for j in range(2):
                sp.sem_inc(sem(f"wst{j}"), 32)

            def store(e, i, ch):
                sp.wait_ge(sem("wsplit"), NCH * i + ch + 1)
                for part, buf in enumerate((whi[:, ch % 2, :].bitcast(F32), wraw[:, ch % 2, :])):
                    half, c = divmod(ch, NCH // 2)
                    sp.dma_start(wsp_d[4 * e + 2 * part + half, :, c * WC:(c + 1) * WC], buf).then_inc(sem(f"wst{ch % 2}"), 16)
                sp.wait_ge(sem(f"wst{ch % 2}"), 32 * (NCH // 2 * i + ch // 2) + 64)

            def expert_split(e, last):
                for ch in range(NCH):
                    store(e, e, ch)
                    if ch + 2 < NCH or not last:
                        load(e + (ch + 2) // NCH, (ch + 2) % NCH)

            EH = E // H
            for h in range(H):
                if h < H - 1:
                    with sp.Fori(0, EH) as i:
                        expert_split(EH * h + i, False)
                else:
                    for e in range(EH * h, E):
                        expert_split(e, e == E - 1)
                if h + 2 < H:
                    sp.wait_ge(sem("pv"), 3 + NP * NB * (h + 1))
                    v_load(h + 2)

            sp.wait_ge(sem("o_ev"), UNITS + 1)
            sp.dma_start(bob[:], bo.partition_broadcast(P)).then_inc(sem("c_bo"), 16)
            sp.dma_start(wot[:], wo_t.rearrange("(k p) n -> p k n", p=P)).then_inc(sem("c_wo"), 16)
            sp.dma_start(rt[:], router_t.rearrange("(k p) n -> p k n", p=P)).then_inc(sem("c_rt"), 16)
            xt = x.rearrange("(t p) d -> t p d", p=P)
            ot = out[0:TOK, :].rearrange("(t p) d -> t p d", p=P)
            xlt = xln_d.rearrange("(t p) d -> t p d", p=P)

            def load_x(s):
                sp.dma_start(xin[:, s.par, :], xt[s.v, :, :]).then_inc(sem(f"xin{s.par}"), 16)

            def io(s, more):
                sp.wait_ge(sem("x2"), s.v + 1)
                sp.dma_start(ot[s.v, :, :], x2[:, s.par, :]).then_inc(sem(f"ox{s.par}"), 16)
                if more:
                    load_x(s.back(-2))
                sp.wait_ge(sem("x3"), s.v + 1)
                sp.dma_start(xlt[s.v, :, :], x3[:, s.par, :]).then_inc(sem(f"ol{s.par}"), 16)

            Wq = W[:].rearrange("p e t (h c) -> p (e t h) c", h=2)

            WF = NT // 2

            def tile_io(s, more):
                io(s, more)
                if s.par == 0:
                    if not (s.i is None and s.off < 2):
                        sp.wait_ge(sem("we"), 16 * s.half)
                        sp.sem_inc(sem("w_in"), 1)
                    sp.dma_start(Wq[:, s.half, :].bitcast(F32), wsp_d[s.half, :, :]).then_inc(sem("we"), 16)

            def load_w(s):
                if not (s.i is None and s.off < WF + 2):
                    sp.wait_ge(sem(f"we{s.par}"), 16 * (s.half - WF // 2))
                    sp.sem_inc(sem("w_in"), 1)
                sp.dma_start(Wq[:, s.v, :].bitcast(F32), wsp_d[s.v, :, :]).then_inc(sem(f"we{s.par}"), 16)

            load_x(Step(None, 0))
            load_x(Step(None, 1))
            run_steps(sp, 0, NT - 2, lambda s: tile_io(s, True))
            for t in (NT - 2, NT - 1):
                tile_io(Step(None, t), False)
            sp.wait_ge(sem("zrow"), 1)
            sp.dma_start(out[TOK:TOK + BLK, :], zrow[:]).then_inc(sem("pad_out"), 16)
            for j in range(2):
                sp.wait_ge(sem(f"ox{j}"), NT // 2 * 16)
                sp.wait_ge(sem(f"ol{j}"), NT // 2 * 16)
            sp.wait_ge(sem("pad_out"), 16)
            sp.sem_inc(sem("rows_out"), 1)
            sp.wait_ge(sem("we"), 16 * WF)
            sp.sem_inc(sem("w_in"), 1)
            load_w(Step(None, WF))
            load_w(Step(None, WF + 1))
            run_steps(sp, WF + 2, 5 * 4, load_w)
            sp.wait_ge(sem("routed"), 1)
            run_steps(sp, 5 * 4, 4 * E, load_w)
            for j in range(2):
                sp.wait_ge(sem(f"we{j}"), 16 * (4 * E - WF) // 2)
                sp.sem_inc(sem("w_in"), 1)

        @block.gpsimd
        def _(pool):
            def held():
                pool.sem_inc(sem("pool_held"), 1)

            pool.memset(ident[:], 0.0).then_inc(sem("id0"), 1)
            pool.memset(ctxt[:, NC - 1, :], 0.0).then_inc(sem("ctx_pad"), 1)
            pool.memset(mcol[:], 0.0).then_inc(sem("mc0"), 1)
            pool.wait_ge(sem("id0"), 1)
            pool.affine_select(out=ident[:], in_=ident[:], compare_op=ALU.not_equal, fill=1.0, base=0,
                               pattern=[[-1, P]], channel_multiplier=1).then_inc(sem("ident"), 1)
            pool.memset(knat[:, :, :, D:D + 1], -1.0).then_inc(sem("kn0"), 1)
            pool.memset(Vs[:, :, :, D:D + 1].bitcast(F32), 1.0).then_inc(sem("v1"), 1)
            pool.memset(qnat[:, :, D:D + 1], 0.0).then_inc(sem("qn0"), 1)
            pool.memset(qnat[:, :, D + 1:D + 2], 1.0).then_inc(sem("qn0"), 1)
            pool.wait_ge(sem("ident"), 1)
            pool.wait_ge(sem("ctx_pad"), 1)
            pool.wait_ge(sem("mc0"), 1)
            pool.wait_ge(sem("kn0"), 1)
            pool.wait_ge(sem("v1"), 1)
            pool.wait_ge(sem("qn0"), 2)
            pool.memset(S2[D:P, :, :].bitcast(F32), 0.0).then_inc(sem("s20"), 1)
            pool.wait_ge(sem("s20"), 1)

            def pro(s, mk, qs):
                if mk:
                    t = s.back(1)
                    if not (t.i is None and t.off < 2):
                        pool.wait_ge(sem("kT_mm"), t.v - 1)
                    pool.wait_ge(sem("mcol"), 1)
                    held()
                    pool.tensor_copy(knat[:, t.par, :, D + 1], mcol[:, bass.ds(t.v, 1)].to_broadcast([P, H]))\
                        .then_inc(sem("kmask"), 1)
                if qs:
                    t = s.back(1 + NC)
                    pool.wait_ge(sem("q_n"), t.v + 1)
                    pool.tensor_tensor(q_by_head[:, :, t.v, 0:D], q_by_head[:, :, t.v, 0:D],
                                       gs[:].unsqueeze(1).to_broadcast([P, H, D]), ALU.mult)\
                        .then_inc(sem("q_s"), 1)

            for lo, hi, a in ((1, NC + 1, (1, 0)), (NC + 1, NK + 1, (1, 1))):
                run_steps(pool, lo, hi, lambda s, a=a: pro(s, *a))

            NCH = EW // WC

            def split(i, ch):
                n = NCH * i + ch
                half = NCH // 2 * i + ch // 2
                pool.wait_ge(sem(f"raw{ch % 2}"), 16 * half + 16)
                pool.wait_ge(sem(f"wst{ch % 2}"), 32 * half + 32)
                held()
                pool.tensor_copy(whi[:, ch % 2, :], wraw[:, ch % 2, :]).then_inc(sem("whi"), 1)
                pool.wait_ge(sem("whi"), n + 1)
                pool.tensor_tensor(wraw[:, ch % 2, :].bitcast(F32R), wraw[:, ch % 2, :],
                                   whi[:, ch % 2, :].bitcast(F32), ALU.subtract).then_inc(sem("wsplit"), 1)

            NG_ = len(POOL_PAIRS)
            SHARE = NCH * E // UNITS
            for h in range(H):
                with pool.Fori(0, NB // 2) as i:
                    for j in range(2):
                        u = NB * h + 2 * i + j
                        for n, p in enumerate(POOL_PAIRS):
                            pool.wait_ge(sem("p_hi"), NP * u + p + 1)
                            pool.tensor_tensor(Pl[:, p % 3, :, :], PT[:, p % 3, :, :],
                                               Ph[:, p % 3, :, :].bitcast(F32), ALU.subtract)\
                                .then_inc(sem("p_lo_g"), 1)
                            for ch in range(SHARE * n // NG_, SHARE * (n + 1) // NG_):
                                split(E // H * h + i, SHARE * j + ch)

            pool.wait_ge(sem("o_ev"), UNITS + 1)
            pool.wait_ge(sem("wst0"), E * NCH // 2 * 32 + 32)
            pool.wait_ge(sem("wst1"), E * NCH // 2 * 32 + 32)

            def gather_heads(s):
                if not (s.i is None and s.off < 2):
                    pool.wait_ge(sem("oT_mm"), s.v - 1)
                held()
                pool.tensor_copy(heads(ost[:, s.par, :]), q_by_head[:, :, s.v, 0:D]).then_inc(sem("ost"), 1)

            run_steps(pool, 0, 4, gather_heads)
            pool.memset(zrow[:], 0.0).then_inc(sem("zrow"), 1)
            pool.iota(iot_i[:], pattern=[[1, P]], base=0, channel_multiplier=0).then_inc(sem("iota"), 1)
            pool.iota(tid_i[:], pattern=[[P, NT]], base=1, channel_multiplier=1).then_inc(sem("iota"), 1)
            pool.iota(pc_i[:], pattern=[[0, 1]], base=TOK + 1, channel_multiplier=1).then_inc(sem("iota"), 1)
            pool.memset(ones[:], 1.0).then_inc(sem("ones"), 1)
            pool.memset(U[:], 1.0).then_inc(sem("u0"), 1)
            pool.wait_ge(sem("u0"), 1)
            pool.affine_select(out=U[:], in_=U[:], compare_op=ALU.is_gt, fill=0.0, base=0,
                               pattern=[[1, P]], channel_multiplier=-1).then_inc(sem("U"), 1)
            run_steps(pool, 4, NT, gather_heads)

            pool.wait_ge(sem("routed"), 1)
            pool.wait_ge(sem("rows_out"), 1)

            def gather(s):
                if not (s.i is None and s.off < 2):
                    pool.wait_ge(sem("xTe_mm"), s.v - 1)
                    pool.wait_ge(sem(f"g_in{s.par}"), 16 * s.half)
                held()
                pool.tensor_copy(ring_g[:, s.par:s.par + 1], gidx[:, bass.ds(s.v, 1)]).then_inc(sem("rg"), 1)
                pool.wait_ge(sem("rg"), s.v + 1)
                held()
                pool.indirect_dma_start(xg[:, s.par, :], None, xln_d,
                                        bass.IndirectOffsetOnAxis(ap=ring_g[:, s.par:s.par + 1], axis=0))\
                    .then_inc(sem(f"g_in{s.par}"), 16)

            def scatter(s):
                pool.wait_ge(sem("ysb"), s.v + 1)
                if not (s.i is None and s.off < 2):
                    pool.wait_ge(sem(f"add{s.par}"), 16 * s.half)
                held()
                pool.tensor_copy(ring_s[:, s.par:s.par + 1], sidx[:, bass.ds(s.v, 1)]).then_inc(sem("rs"), 1)
                pool.wait_ge(sem("rs"), s.v + 1)
                if not (s.i is None and s.off < 1):
                    b = s.back(1)
                    pool.wait_ge(sem(f"add{b.par}"), 16 * b.half + 16)
                held()
                pool.indirect_dma_start(out, bass.IndirectOffsetOnAxis(ap=ring_s[:, s.par:s.par + 1], axis=0),
                                        ysb[:, s.par, :], None, compute_op=ALU.add)\
                    .then_inc(sem(f"add{s.par}"), 16)

            def step(s, g, sc):
                if g:
                    gather(s)
                if sc:
                    scatter(s.back(3))

            for lo, hi, a in ((0, 3, (1, 0)), (3, NBLK, (1, 1)), (NBLK, NBLK + 3, (0, 1))):
                run_steps(pool, lo, hi, lambda s, a=a: step(s, *a))
            for j in range(2):
                pool.wait_ge(sem(f"add{j}"), 16 * ((NBLK + 1 - j) // 2))

        @block.scalar
        def _(act):
            act.dma_start(wc[0:P, 0, :], w_ctx[0:P, :]).then_inc(sem("wc_in"), 16)
            act.dma_start(wc[0:CIN - P, 1, :], w_ctx[P:CIN, :]).then_inc(sem("wc_in2"), 16)
            gains = ((ln_x_g, CIN), (ln_x_b, CIN), (ln_l_g, DIM), (ln_l_b, DIM))
            for n, (g, w) in enumerate(gains):
                for k in range(2):
                    r = min(P, w - k * P)
                    act.dma_start(cols[0:r, 2 * n + k:2 * n + k + 1],
                                  g[k * P:k * P + r].rearrange("(p a) -> p a", a=1)).then_inc(sem("cols"), 16)
            act.dma_start(gq[:, 0, :], qn_g.partition_broadcast(P)).then_inc(sem("gq"), 16)
            act.dma_start(gq[:, 1, :], kn_g.partition_broadcast(P)).then_inc(sem("gq"), 16)
            act.dma_start(m_u8[:, 0:NC - 1], mask[0:(NC - 1) * P].rearrange("(t p) -> p t", p=P),
                          allow_slow_non_contiguous=True).then_inc(sem("m_in"), 16)
            act.dma_start(m_u8[0:CTX - (NC - 1) * P, NC - 1:NC],
                          mask[(NC - 1) * P:CTX].rearrange("(p a) -> p a", a=1)).then_inc(sem("m_in"), 16)

            act.wait_ge(sem("bn"), NC)
            act.activation(sda[:, 0:NC], mvs[:, 0:NC, 1], ACT.Sqrt, bias=eps[:, 0:1]).then_inc(sem("sd_c"), 1)

            def pro(s, b, c):
                if b:
                    t = s.back(2)
                    lo = 0 if b == 'l' else DIM
                    act.wait_ge(sem("qk_mm"), t.v + 1)
                    if not (t.i is None and t.off < 1):
                        act.wait_ge(sem("ss"), t.v)
                    act.activation(bSq[:, 0, lo:2 * DIM], bA[t.par][:, 0, lo:2 * DIM], ACT.Square)\
                        .then_inc(sem("sq"), 1)
                kT = bK[0:A, 0, :].rearrange("p (h c) -> p h c", h=H)
                if c:
                    c_ = s.back(4)
                    act.wait_ge(sem("kT_mm"), c_.v + 1)
                    act.copy(S2[0:A, :, bass.ds(c_.v * P, P)], kT).then_inc(sem("s2"), 1)
                if b:
                    act.wait_ge(sem("v_mm"), t.v + 1)
                    if not (t.i is None and t.off < 2):
                        act.wait_ge(sem(f"v_st{t.par}"), 16 * t.half)
                    act.copy(Vs[:, t.par, :, 0:D], heads(bV[t.par][:, 0, 0:DIM])).then_inc(sem("v_hi"), 1)
                    lo = 0 if b == 'l' else H
                    act.wait_ge(sem("ss"), t.v + 1)
                    act.activation(nrm[:, lo:2 * H], ss[:, lo:2 * H], ACT.Sqrt, scale=1.0 / D)\
                        .then_inc(sem("nrm"), 1)
                if c:
                    act.wait_ge(sem("s2"), c_.v + 1)
                    act.copy(S1[0:D, :, bass.ds(c_.v * P, P)],
                             S2[0:D, :, bass.ds(c_.v * P, P)].bitcast(F32)).then_inc(sem("s1"), 1)

            def lat_sd():
                act.wait_ge(sem("bn"), NK)
                act.activation(sda[:, NC:NK], mvs[:, NC:NK, 1], ACT.Sqrt, bias=eps[:, 0:1]).then_inc(sem("sd_l"), 1)
                act.wait_ge(sem("v2"), 1)
                act.activation(sda[:, NC:NK], va[:, NC:NK], ACT.Sqrt, bias=eps[:, 0:1]).then_inc(sem("sd_l"), 1)

            act.wait_ge(sem("v1"), 1)
            act.wait_ge(sem("s20"), 1)
            run_steps(act, 2, 4, lambda s: pro(s, 'c', 0))
            run_steps(act, 4, LAT_AT + 2, lambda s: pro(s, 'c', 1))
            lat_sd()
            for lo, hi, a in ((LAT_AT + 2, NC + 2, ('c', 1)), (NC + 2, NK + 2, ('l', 1)), (NK + 2, NK + 4, (0, 1))):
                run_steps(act, lo, hi, lambda s, a=a: pro(s, *a))

            act.sem_inc(sem("exp"), 2)
            act.wait_ge(sem("klo"), NK)
            act.wait_ge(sem("q_s"), NT)
            act.wait_ge(sem("q1w"), 1)
            act.wait_ge(sem("q20"), 1)

            def q_evac(v, par):
                act.wait_ge(sem("qT_mm"), v + 1)
                act.copy(Q2[0:A, par, :], bT[0:A, 0, :]).then_inc(sem("q2"), 1)

            def q_evac_1(v, par):
                act.copy(Q1[D:2 * D, par, :], bT[0:D, 0, :]).then_inc(sem("q1h"), 1)

            def c_row(v, par):
                act.wait_ge(sem("cT_mm"), v + 1)
                act.copy(Q2[D:D + 1, par, :], bT[0:1, 0, :]).then_inc(sem("c_row"), 1)

            def unit(u, j):
                for p in range(NP):
                    g = NP * u + p
                    w = 2 if 2 * p + 1 < NK else 1
                    sl = (NP * j + p) % 2
                    act.wait_ge(sem("s_mm"), g + 1)
                    act.wait_ge(sem("pv"), g + 1)
                    act.activation(PT[:, p % 3, 0:w, :], bS[sl][:, 0:w, :], ACT.Exp).then_inc(sem("exp"), 1)
                    if p == 1:
                        q_evac(u + 1, (j + 1) % 2)
                    if p == 2:
                        q_evac_1(u + 1, (j + 1) % 2)
                    act.wait_ge(sem("exp"), g + 3)
                    act.copy(Ph[:, p % 3, 0:w, :], PT[:, p % 3, 0:w, :]).then_inc(sem("p_hi"), 1)
                c_row(u + 1, (j + 1) % 2)
                act.wait_ge(sem("pv"), NP * (u + 1) + 3)
                act.wait_ge(sem("oT_a"), u + 1)
                act.copy(oT_a[0:D + 1, :], bPV[0:D + 1, 0, :]).then_inc(sem("o_cp"), 1)

            q_evac(0, 0)
            q_evac_1(0, 0)
            c_row(0, 0)
            for h in range(H):
                with act.Fori(0, NB // 2) as i:
                    for j in range(2):
                        unit(NB * h + 2 * i + j, j)

            def fin(s, a, b, c):
                if a:
                    act.wait_ge(sem("oT_mm"), s.v + 1)
                    if not (s.i is None and s.off < 2):
                        act.wait_ge(sem("y_mm"), s.v - 1)
                    act.copy(oT[:, s.par, :, :], bFT[s.par][:, 0, 0:DIM].rearrange("p (k c) -> p k c", k=2))\
                        .then_inc(sem("oT"), 1)
                if c:
                    t = s.back(4)
                    act.wait_ge(sem("x3T_mm"), t.v + 1)
                    if not (t.i is None and t.off < 2):
                        act.wait_ge(sem("lg_mm"), t.v - 1)
                    act.copy(x3T[:, t.par, :, :], bFX[t.par][:, 0, 0:DIM].rearrange("p (k c) -> p k c", k=2))\
                        .then_inc(sem("x3T"), 1)
                if b:
                    t = s.back(2)
                    act.wait_ge(sem("mv2"), t.v + 1)
                    if not (t.i is None and t.off < 2):
                        act.wait_ge(sem("rs2"), t.v - 1)
                    act.activation(sd2[:, t.par:t.par + 1], mv2[:, t.par, 1:2], ACT.Sqrt, bias=eps[:, 0:1])\
                        .then_inc(sem("sd2"), 1)

            for lo, hi, a in ((0, 2, (1, 0, 0)), (2, 4, (1, 1, 0)), (4, NT, (1, 1, 1)), (NT, NT + 2, (0, 1, 1)),
                              (NT + 2, NT + 4, (0, 0, 1))):
                run_steps(act, lo, hi, lambda s, a=a: fin(s, *a))
            act.wait_ge(sem("r_sh"), 1)
            act.activation(ra[:], rb[:], ACT.Exp).then_inc(sem("r_ex"), 1)

            def ffn(s, x_, g, h):
                if h:
                    t = s.back(2)
                    act.wait_ge(sem("hT_mm"), t.v + 1)
                    if not (t.i is None and t.off < 1):
                        act.wait_ge(sem("y_e"), t.v)
                    act.copy(hTe[:, 0, :, :], bH[:, 0, :].rearrange("p (k c) -> p k c", k=I // P))\
                        .then_inc(sem("hhi"), 1)
                if g:
                    t = s.back(1)
                    act.wait_ge(sem("g_mm"), t.v + 1)
                    if not (t.i is None and t.off < 1):
                        act.wait_ge(sem("hT_mm"), t.v)
                    act.activation(hs[:], bG[t.par][:, 0, :], ACT.Silu).then_inc(sem("silu"), 1)
                if x_:
                    act.wait_ge(sem("xTe_mm"), s.v + 1)
                    if not (s.i is None and s.off < 2):
                        act.wait_ge(sem("u_mm"), s.v - 1)
                    act.copy(xTe[:, s.par, 0, :, :], bXe[:, 0, 0:DIM].rearrange("p (k c) -> p k c", k=2))\
                        .then_inc(sem("xhi"), 1)

            for lo, hi, a in FFN_SEGMENTS:
                run_steps(act, lo, hi, lambda s, a=a: ffn(s, *a))

        @block.vector
        def _(dve):
            link_n = [0]

            def link(ins):
                link_n[0] += 1
                ins.then_inc(sem("link"), 1)
                dve.wait_ge(sem("link"), link_n[0])

            dve.memset(eps[:], LN_EPS).then_inc(sem("eps"), 1)
            dve.memset(xT[CIN - P:P, :, 1, :], 0.0).then_inc(sem("xT0"), 1)
            dve.memset(wc[CIN - P:P, 1, :], 0.0).then_inc(sem("wc0"), 1)
            def stats(src, t):
                dve.bn_stats(st6[:, t, :], src).then_inc(sem("bn0"), 1)

            def aggregate(lo, hi):
                for t in range(lo, hi):
                    dve.wait_ge(sem("bn0"), t + 1)
                    dve.bn_aggr(mvs[:, t, :], st6[:, t, :]).then_inc(sem("bn"), 1)

            for n, (lo, hi) in enumerate(CTX_LOADS):
                dve.wait_ge(sem(f"ctx_in{n}"), 16)
                for t in range(lo, hi):
                    stats(ctxt[:, t, :], t)
            dve.wait_ge(sem("ctx_in_l"), 16)
            stats(ctxt[:, NC - 1, :], NC - 1)
            aggregate(0, NC)
            dve.wait_ge(sem("sd_c"), 1)
            link(dve.reciprocal(rsd[:, 0:NC], sda[:, 0:NC]))

            def apply(t, kind):
                src = ctxt[:, t.v, :] if kind == 'c' else xall[:, t.back(NC).v, :]
                w = CIN if kind == 'c' else DIM
                if not (t.i is None and t.off < 2):
                    dve.wait_ge(sem("xT_mm"), t.v - 1)
                dve.tensor_scalar(xn[:, t.par, 0:w], src, mvs[:, t.v, 0:1], rsd[:, bass.ds(t.v, 1)],
                                  ALU.subtract, ALU.mult).then_inc(sem("ln"), 1)

            def pro(s, a, ln, b, c):
                if a:
                    dve.wait_ge(sem("xT_mm"), s.v + 1)
                    if not (s.i is None and s.off < 2):
                        dve.wait_ge(sem("v_mm"), s.v - 1)
                    for k in range(2):
                        r = P if (k == 0 or a == 'l') else CIN - P
                        g0 = 0 if a == 'c' else 4
                        dve.tensor_scalar(xT[0:r, s.par, k, :], bX[s.par][0:r, 0, k * P:(k + 1) * P],
                                          cols[0:r, g0 + k:g0 + k + 1], cols[0:r, g0 + 2 + k:g0 + 3 + k],
                                          ALU.mult, ALU.add).then_inc(sem("xT"), 1)
                if ln:
                    apply(s.back(-1), ln)
                if b:
                    t = s.back(2)
                    lo = 0 if b == 'l' else H
                    dve.wait_ge(sem("sq"), t.v + 1)
                    dve.tensor_reduce(ss[:, lo:2 * H], heads(bSq[:, 0, lo * D:2 * DIM]), AX, ALU.add)\
                        .then_inc(sem("ss"), 1)
                if c:
                    c_ = s.back(4)
                    dve.wait_ge(sem("s2"), c_.v + 1)
                    dve.tensor_tensor(S1[D:2 * D, :, bass.ds(c_.v * P, P)],
                                      bK[0:D, 0, :].rearrange("p (h c) -> p h c", h=H),
                                      S2[0:D, :, bass.ds(c_.v * P, P)].bitcast(F32), ALU.subtract)\
                        .then_inc(sem("klo"), 1)
                if b:
                    dve.wait_ge(sem("v_hi"), t.v + 1)
                    dve.tensor_tensor(Vs[:, t.par, :, D + 1:VW], heads(bV[t.par][:, 0, 0:DIM]),
                                      Vs[:, t.par, :, 0:D].bitcast(F32), ALU.subtract).then_inc(sem("v_lo"), 1)
                    dve.wait_ge(sem("nrm"), t.v + 1)
                    dve.tensor_scalar(rn0[:, lo:2 * H], nrm[:, lo:2 * H], RMS_EPS, None, ALU.max)\
                        .then_inc(sem("rn0"), 1)
                    dve.wait_ge(sem("rn0"), t.v + 1)
                    dve.reciprocal(rn[:, lo:2 * H], rn0[:, lo:2 * H]).then_inc(sem("rn"), 1)
                    dve.wait_ge(sem("rn"), t.v + 1)
                    if b == 'l':
                        dve.tensor_tensor(q_by_head[:, :, t.back(NC).v, 0:D], heads(bA[t.par][:, 0, 0:DIM]),
                                          rn[:, 0:H].unsqueeze(2).to_broadcast([P, H, D]), ALU.mult)\
                            .then_inc(sem("q_n"), 1)
                    if not (t.i is None and t.off < 2):
                        dve.wait_ge(sem("kT_mm"), t.v - 1)
                    dve.tensor_tensor(knat[:, t.par, :, 0:D], heads(bA[t.par][:, 0, DIM:2 * DIM]),
                                      rn[:, H:2 * H].unsqueeze(2).to_broadcast([P, H, D]), ALU.mult)\
                        .then_inc(sem("knat"), 1)

            apply(Step(None, 0), 'c')
            dve.wait_ge(sem("m_in"), 32)
            dve.wait_ge(sem("mc0"), 1)
            NF = NC - 1
            link(dve.tensor_scalar(mcol[:, 0:NF], m_u8[:, 0:NF], -1.0, BIG, ALU.add, ALU.mult))
            link(dve.memset(mcol[:, NF:NC], -BIG))
            dve.tensor_scalar(mcol[0:CTX - NF * P, NF:NC], m_u8[0:CTX - NF * P, NF:NC], -1.0, BIG, ALU.add, ALU.mult)\
                .then_inc(sem("mcol"), 1)
            dve.wait_ge(sem("gq"), 32)
            dve.scalar_tensor_tensor(gs[:], gq[:, 0, :], SCALE, gq[:, 1, :], ALU.mult, ALU.mult)\
                .then_inc(sem("gs"), 1)
            dve.wait_ge(sem("cols"), 128)
            dve.wait_ge(sem("xT0"), 1)
            dve.wait_ge(sem("v1"), 1)
            run_steps(dve, 0, 2, lambda s: pro(s, 'c', 'c', 0, 0))
            run_steps(dve, 2, 4, lambda s: pro(s, 'c', 'c', 'c', 0))
            run_steps(dve, 4, LAT_AT + 1, lambda s: pro(s, 'c', 'c', 'c', 1))
            dve.wait_ge(sem("x_in"), 16)
            for t in range(NT):
                stats(xall[:, t, :], NC + t)
            aggregate(NC, NK)
            run_steps(dve, LAT_AT + 1, LAT_AT + 2, lambda s: pro(s, 'c', 'c', 'c', 1))
            L = slice(NC, NK)
            dve.wait_ge(sem("sd_l"), 1)
            link(dve.reciprocal(rsd[:, L], sda[:, L]))
            link(dve.tensor_tensor(va[:, L], rsd[:, L], rsd[:, L], ALU.mult))
            dve.tensor_tensor(va[:, L], va[:, L], mvs[:, L, 1], ALU.mult).then_inc(sem("v2"), 1)
            dve.wait_ge(sem("sd_l"), 2)
            link(dve.reciprocal(va[:, L], sda[:, L]))
            link(dve.tensor_tensor(rsd[:, L], rsd[:, L], va[:, L], ALU.mult))
            for lo, hi, a in ((LAT_AT + 2, NC - 1, ('c', 'c', 'c', 1)), (NC - 1, NC, ('c', 'l', 'c', 1)),
                              (NC, NC + 2, ('l', 'l', 'c', 1)), (NC + 2, NK - 1, ('l', 'l', 'l', 1)),
                              (NK - 1, NK, ('l', 0, 'l', 1)), (NK, NK + 2, (0, 0, 'l', 1)),
                              (NK + 2, NK + 4, (0, 0, 0, 1))):
                run_steps(dve, lo, hi, lambda s, a=a: pro(s, *a))

            dve.wait_ge(sem("q_s"), NT)
            dve.wait_ge(sem("s1"), NK)
            dve.wait_ge(sem("nrm"), NK)
            for j in range(2):
                dve.wait_ge(sem(f"v_st{j}"), (NK + 1 - j) // 2 * 16)
            dve.memset(cmax[:], 0.0).then_inc(sem("q1w"), 1)
            dve.memset(Q2[D:P, :, :].bitcast(F32), 0.0).then_inc(sem("q20"), 1)
            dve.memset(oT_a[:], 1.0).then_inc(sem("o_cp"), 1)

            def q_stage(v, src):
                if not isinstance(v, int) or v:
                    dve.wait_ge(sem("qT_mm"), v)
                dve.tensor_copy(qst[:], qnat[:, bass.ds(QB + src * QB, QB), :]).then_inc(sem("qst"), 1)

            def q_lo(v, par):
                dve.wait_ge(sem("q2"), v + 1)
                dve.wait_ge(sem("q1h"), v + 1)
                dve.tensor_tensor(Q1[0:D, par, :], bT[0:D, 0, :], Q2[0:D, par, :].bitcast(F32), ALU.subtract)\
                    .then_inc(sem("q_lo"), 1)

            def piece(v, k, banks):
                i, g = divmod(k, NG)
                dve.wait_ge(sem("m_mm"), NM * v + k + 1)
                dve.tensor_reduce(mpart[:, i, g:g + 1], banks[k % len(banks)][:, 0:PIECE], AX, ALU.max)\
                    .then_inc(sem("m_red"), 1)

            def pieces(v, at):
                for n in (2 * SLOTS.index(at), 2 * SLOTS.index(at) + 1) if at in SLOTS else ():
                    piece(v, n, M_BANKS)

            def maxima(v):
                dve.wait_ge(sem("m_red"), NM * v + NM)
                if not isinstance(v, int) or v:
                    dve.wait_ge(sem("cT_mm"), v)
                dve.tensor_reduce(cmax[:], mpart[:], AX, ALU.max).then_inc(sem("cmax"), 1)

            def o_out(v):
                dve.wait_ge(sem("oT_a"), v + 1)
                o = bT[:, 0, 0:QB * (D + 1)].rearrange("p (i d) -> p i d", i=QB)
                dve.reciprocal(orec[:], o[:, :, D]).then_inc(sem("orec"), 1)
                dve.wait_ge(sem("orec"), v + 1)
                dve.tensor_tensor(qnat[:, bass.ds(v * QB, QB), 0:D], o[:, :, 0:D],
                                  orec[:].unsqueeze(2).to_broadcast([P, QB, D]), ALU.mult).then_inc(sem("o_ev"), 1)

            def p_lo(u, p):
                w = 2 if 2 * p + 1 < NK else 1
                if p in POOL_PAIRS:
                    return
                dve.wait_ge(sem("p_hi"), NP * u + p + 1)
                dve.tensor_tensor(Pl[:, p % 3, 0:w, :], PT[:, p % 3, 0:w, :],
                                  Ph[:, p % 3, 0:w, :].bitcast(F32), ALU.subtract).then_inc(sem("p_lo"), 1)

            def unit(u, j, last):
                q_stage(u + 1, (u + 1) % UNITS if last else u + 1)
                for p in range(NP):
                    pieces(u + 1, (p, 0))
                    if p:
                        p_lo(u, p - 1)
                    if p == 2:
                        q_lo(u + 1, (j + 1) % 2)
                    if p == 4:
                        o_out(u)
                    pieces(u + 1, (p, 1))
                    pieces(u + 1, (p, 2))
                    if p == SLOTS[-1][0]:
                        maxima(u + 1)
                p_lo(u, NP - 1)

            dve.wait_ge(sem("q1w"), 1)
            q_stage(0, 0)
            q_lo(0, 0)
            for k in range(NM):
                piece(0, k, FIRST_BANKS)
            maxima(0)
            for h in range(H):
                with dve.Fori(0, NB // 2) as i:
                    for j in range(2):
                        unit(NB * h + 2 * i + j, j, h == H - 1 and j == 1)
            o_out(UNITS)

            dve.wait_ge(sem("wst0"), E * (EW // WC) // 2 * 32 + 32)
            dve.wait_ge(sem("wst1"), E * (EW // WC) // 2 * 32 + 32)
            dve.wait_ge(sem("o_ev"), UNITS + 1)
            dve.wait_ge(sem("c_bo"), 16)

            def fin(s, b, c, d):
                if b:
                    t = s.back(2)
                    dve.wait_ge(sem(f"xin{t.par}"), 16 * t.half + 16)
                    if not (t.i is None and t.off < 2):
                        dve.wait_ge(sem(f"ox{t.par}"), 16 * t.half)
                        dve.wait_ge(sem("x3"), t.v - 1)
                    dve.tensor_tensor(x2[:, t.par, :], xin[:, t.par, :], bob[:], ALU.add).then_inc(sem("xb"), 1)
                    dve.wait_ge(sem("xb"), t.v + 1)
                    dve.wait_ge(sem("y_mm"), t.v + 1)
                    dve.tensor_tensor(x2[:, t.par, :], x2[:, t.par, :], bFY[t.par][:, 0, 0:DIM], ALU.add)\
                        .then_inc(sem("x2"), 1)
                if c:
                    q = s.back(3)
                    dve.wait_ge(sem("sd2"), q.v + 1)
                    if not (q.i is None and q.off < 1):
                        dve.wait_ge(sem("x3"), q.v)
                    dve.reciprocal(rs2[:], sd2[:, q.par:q.par + 1]).then_inc(sem("rs2"), 1)
                    dve.wait_ge(sem("rs2"), q.v + 1)
                    dve.wait_ge(sem("mv2"), q.v + 1)
                    if not (q.i is None and q.off < 2):
                        dve.wait_ge(sem(f"ol{q.par}"), 16 * q.half)
                        dve.wait_ge(sem("x3T_mm"), q.v - 1)
                    dve.tensor_scalar(x3[:, q.par, :], x2[:, q.par, :], mv2[:, q.par, 0:1], rs2[:, 0:1],
                                      ALU.subtract, ALU.mult).then_inc(sem("x3"), 1)
                if b:
                    dve.wait_ge(sem("x2"), t.v + 1)
                    if not (t.i is None and t.off < 1):
                        dve.wait_ge(sem("mv2"), t.v)
                    dve.bn_stats(st2[:], x2[:, t.par, :]).then_inc(sem("st2"), 1)
                    dve.wait_ge(sem("st2"), t.v + 1)
                    dve.sem_inc(sem("dve_held"), 1)
                    dve.bn_aggr(mv2[:, t.par, :], st2[:]).then_inc(sem("mv2"), 1)
                if d:
                    q = s.back(5)
                    dve.wait_ge(sem("lg_mm"), q.v + 1)
                    dve.tensor_copy(lg[:, q.v, :], bL[:, 0, 0:E]).then_inc(sem("lg"), 1)

            for lo, hi, a in ((2, 3, (1, 0, 0)), (3, 5, (1, 1, 0))):
                run_steps(dve, lo, hi, lambda s, a=a: fin(s, *a))
            dve.wait_ge(sem("iota"), 3)
            link(dve.tensor_copy(iot[:], iot_i[:]))
            link(dve.tensor_copy(tid[:], tid_i[:]))
            link(dve.tensor_copy(pc[:], pc_i[:]))
            link(dve.tensor_scalar(thr[:], iot[:, 0:NBLK + 1], float(P), None, ALU.mult))
            link(dve.tensor_scalar(w8[:], iot[:, 0:E], -1.0, float(E), ALU.mult, ALU.add))
            for lo, hi, a in ((5, NT + 2, (1, 1, 1)),
                              (NT + 2, NT + 3, (0, 1, 1)), (NT + 3, NT + 5, (0, 0, 1))):
                run_steps(dve, lo, hi, lambda s, a=a: fin(s, *a))

            def over_e(ap):
                return ap.unsqueeze(2).to_broadcast([P, NT, E])

            dve.wait_ge(sem("lg"), NT)
            link(dve.tensor_reduce(sm[:], lg[:], AX, ALU.max))
            dve.tensor_tensor(rb[:], lg[:], over_e(sm[:]), ALU.subtract).then_inc(sem("r_sh"), 1)
            dve.wait_ge(sem("r_ex"), 1)
            link(dve.tensor_reduce(sm[:], ra[:], AX, ALU.add))
            link(dve.reciprocal(sm[:], sm[:]))
            link(dve.tensor_tensor(pr[:], ra[:], over_e(sm[:]), ALU.mult))
            w8b = w8[:].unsqueeze(1).to_broadcast([P, NT, E])
            for k in range(2):
                link(dve.tensor_reduce(top_p[:, k, :], pr[:], AX, ALU.max))
                link(dve.tensor_tensor(ra[:], pr[:], over_e(top_p[:, k, :]), ALU.is_equal))
                link(dve.tensor_tensor(ra[:], ra[:], w8b, ALU.mult))
                link(dve.tensor_reduce(sm[:], ra[:], AX, ALU.max))
                link(dve.tensor_tensor(oh[:, k, :, :], w8b, over_e(sm[:]), ALU.is_equal))
                if k == 0:
                    link(dve.scalar_tensor_tensor(pr[:], oh[:, 0, :, :], -2.0, pr[:], ALU.mult, ALU.add))
            dve.tensor_tensor(M[:], oh[:, 0, :, :], oh[:, 1, :, :], ALU.add).then_inc(sem("M"), 1)
            link(dve.tensor_tensor(sm[:], top_p[:, 0, :], top_p[:, 1, :], ALU.add))
            link(dve.tensor_scalar(sm[:], sm[:], 1e-6, None, ALU.add))
            link(dve.reciprocal(sm[:], sm[:]))
            link(dve.tensor_tensor(wgt[:], top_p[:], sm[:].unsqueeze(1).to_broadcast([P, 2, NT]), ALU.mult))

            dve.wait_ge(sem("tot_mm"), 1)
            link(dve.tensor_copy(tot[:], bR[:, 0, P:2 * P].rearrange("p (t e) -> p t e", e=E)))
            link(dve.tensor_copy(ra[:], tot[:]))
            a_, b_ = ra, rb
            k = 1
            while k < NT:
                link(dve.tensor_copy(b_[:, 0:k, :], a_[:, 0:k, :]))
                link(dve.tensor_tensor(b_[:, k:NT, :], a_[:, k:NT, :], a_[:, 0:NT - k, :], ALU.add))
                a_, b_ = b_, a_
                k *= 2
            link(dve.tensor_copy(cs[:, 0, :], a_[:, NT - 1, :]))
            link(dve.tensor_tensor(cmp8[:], cs[:, 0, :].unsqueeze(2).to_broadcast([P, E, NT]),
                                   thr[:, 0:NT].unsqueeze(1).to_broadcast([P, E, NT]), ALU.is_gt))
            link(dve.tensor_reduce(nb[:], cmp8[:], AX, ALU.add))
            link(dve.tensor_copy(cs[:, 0, :], nb[:]))
            c = 0
            k = 1
            while k < E:
                link(dve.tensor_copy(cs[:, 1 - c, 0:k], cs[:, c, 0:k]))
                link(dve.tensor_tensor(cs[:, 1 - c, k:E], cs[:, c, k:E], cs[:, c, 0:E - k], ALU.add))
                c = 1 - c
                k *= 2
            link(dve.tensor_tensor(st128[:], cs[:, c, :], nb[:], ALU.subtract))
            link(dve.tensor_scalar(st128[:], st128[:], float(P), None, ALU.mult))
            link(dve.tensor_tensor(a_[:], a_[:], tot[:], ALU.subtract))
            link(dve.tensor_tensor(a_[:], a_[:], st128[:].unsqueeze(1).to_broadcast([P, NT, E]), ALU.add))
            link(dve.tensor_tensor(a_[:], a_[:], bR[:, 0, 0:P].rearrange("p (t e) -> p t e", e=E), ALU.add))
            for k in range(2):
                link(dve.tensor_tensor(b_[:], oh[:, k, :, :], a_[:], ALU.mult))
                link(dve.tensor_reduce(pos[:, k, :], b_[:], AX, ALU.add))
            flat = pos[:].rearrange("p k t -> p (k t)")
            R = 2 * NT
            link(dve.tensor_tensor(G[:], flat.unsqueeze(2).to_broadcast([P, R, NBLK + 1]),
                                   thr[:].unsqueeze(1).to_broadcast([P, R, NBLK + 1]), ALU.is_ge))
            link(dve.tensor_reduce(rr[:].rearrange("p k t -> p (k t)"), G[:], AX, ALU.add))
            link(dve.scalar_tensor_tensor(rr[:], rr[:], -float(P), pos[:], ALU.mult, ALU.add))
            link(dve.tensor_scalar(rr[:], rr[:], float(P), None, ALU.add))
            link(dve.tensor_tensor(mov[:, :, 1, :], G[:, :, 0:NBLK], G[:, :, 1:NBLK + 1], ALU.subtract))
            for k in range(2):
                link(dve.tensor_tensor(mov[:, k * NT:(k + 1) * NT, 0, :], mov[:, k * NT:(k + 1) * NT, 1, :],
                                       tid[:].unsqueeze(2).to_broadcast([P, NT, NBLK]), ALU.mult))
            link(dve.tensor_tensor(mov[:, :, 1, :], mov[:, :, 1, :],
                                   wgt[:].rearrange("p k t -> p (k t)").unsqueeze(2).to_broadcast([P, R, NBLK]),
                                   ALU.mult))
            rrf = rr[:].rearrange("p k t -> p (k t)")
            for k in range(0, R, OHR):
                dve.tensor_tensor(ohr[:, k:k + OHR, :], iot[:].unsqueeze(1).to_broadcast([P, OHR, P]),
                                  rrf[:, k:k + OHR].unsqueeze(2).to_broadcast([P, OHR, P]), ALU.is_equal)\
                    .then_inc(sem("ohr"), 1)
            link(dve.tensor_tensor(ecmp[:], iot[:, 0:NBLK].unsqueeze(2).to_broadcast([P, NBLK, E - 1]),
                                   cs[:, c, 0:E - 1].unsqueeze(1).to_broadcast([P, NBLK, E - 1]), ALU.is_ge))
            link(dve.tensor_reduce(ef[:], ecmp[:], AX, ALU.add))
            link(dve.tensor_copy(zt[:], ef[:]))
            w = NBLK - 1
            link(dve.scalar_tensor_tensor(zt[:, 0:w], ef[:, 1:NBLK], float(E), ef[:, 0:w], ALU.mult, ALU.add))
            w = NBLK - 2
            link(dve.scalar_tensor_tensor(zt[:, 0:w], ef[:, 2:NBLK], float(E * E), zt[:, 0:w], ALU.mult, ALU.add))
            link(dve.tensor_copy(eid[:], zt[:]))
            dve.wait_ge(sem("tab_mm"), 1)
            link(dve.tensor_copy(tok[:], bR[:, 0, 256:256 + NBLK]))
            link(dve.tensor_copy(wtab[:], bR[:, 0, 256 + NBLK:256 + 2 * NBLK]))
            link(dve.tensor_scalar(gidx[:], tok[:], -1.0, 0.0, ALU.add, ALU.max))
            link(dve.tensor_scalar(zt[:], tok[:], 0.0, pc[:, 0:1], ALU.is_equal, ALU.mult))
            dve.scalar_tensor_tensor(sidx[:], tok[:], -1.0, zt[:], ALU.add, ALU.add).then_inc(sem("routed"), 1)

            def ffn(s, x_, g, h):
                if h:
                    t = s.back(2)
                    dve.wait_ge(sem("hhi"), t.v + 1)
                    dve.tensor_tensor(hTe[:, 1, :, :], bH[:, 0, :].rearrange("p (k c) -> p k c", k=I // P),
                                      hTe[:, 0, :, :].bitcast(F32), ALU.subtract).then_inc(sem("hlo"), 1)
                if g:
                    t = s.back(1)
                    dve.wait_ge(sem("silu"), t.v + 1)
                    dve.wait_ge(sem("u_mm"), t.v + 1)
                    dve.tensor_tensor(hs[:], hs[:], bU[t.par][:, 0, :], ALU.mult).then_inc(sem("hs"), 1)
                if x_:
                    dve.wait_ge(sem("xhi"), s.v + 1)
                    dve.tensor_tensor(xTe[:, s.par, 1, :, :],
                                      bXe[:, 0, 0:DIM].rearrange("p (k c) -> p k c", k=2),
                                      xTe[:, s.par, 0, :, :].bitcast(F32), ALU.subtract).then_inc(sem("xlo"), 1)
                if h:
                    t = s.back(2)
                    dve.wait_ge(sem("y_e"), t.v + 1)
                    if not (t.i is None and t.off < 2):
                        dve.wait_ge(sem(f"add{t.par}"), 16 * t.half)
                    dve.tensor_scalar(ysb[:, t.par, :], bY[:, 0, 0:DIM], wtab[:, bass.ds(t.v, 1)], None, ALU.mult)\
                        .then_inc(sem("ysb"), 1)

            for lo, hi, a in FFN_SEGMENTS:
                run_steps(dve, lo, hi, lambda s, a=a: ffn(s, *a))

        @block.tensor
        def _(pe):
            pe.wait_ge(sem("ident"), 1)

            def pro(s, c, a, b):
                if a:
                    pe.wait_ge(sem("ln"), s.v + 1)
                    for k in range(2):
                        r = P if (k == 0 or a == 'l') else CIN - P
                        last = pe.transpose(bX[s.par][0:r, 0, k * P:(k + 1) * P],
                                            xn[:, s.par, k * P:k * P + r], ident[:])
                    last.then_inc(sem("xT_mm"), 1)
                if b:
                    t = s.back(1)
                    pe.wait_ge(sem("xT"), 2 * t.v + 2)
                    if not (t.i is None and t.off < 2):
                        pe.wait_ge(sem("v_lo"), t.v - 1)
                        pe.wait_ge(sem("knat"), t.v - 1)
                    w, lo = (wl, 0) if b == 'l' else (wc, DIM)
                    n = 2 * DIM - lo
                    for k in range(2):
                        last = pe.matmul(bA[t.par][:, 0, lo:2 * DIM], xT[:, t.par, k, :], w[:, k, 0:n],
                                         start=k == 0, stop=k == 1)
                    last.then_inc(sem("qk_mm"), 1)
                    for k in range(2):
                        last = pe.matmul(bV[t.par][:, 0, 0:DIM], xT[:, t.par, k, :], w[:, k, n:n + DIM],
                                         start=k == 0, stop=k == 1)
                    last.then_inc(sem("v_mm"), 1)
                if c:
                    t = s.back(3)
                    pe.wait_ge(sem("knat"), t.v + 1)
                    pe.wait_ge(sem("kmask"), t.v + 1)
                    if not (t.i is None and t.off < 1):
                        pe.wait_ge(sem("s2"), t.v)
                        pe.wait_ge(sem("klo"), t.v)
                    for h in range(H):
                        last = pe.transpose(bK[0:A, 0, h * P:(h + 1) * P], knat[:, t.par, h, :], ident[:])
                    last.then_inc(sem("kT_mm"), 1)

            pe.wait_ge(sem("kn0"), 1)
            run_steps(pe, 0, 1, lambda s: pro(s, 0, 'c', 0))
            pe.wait_ge(sem("wc_in"), 16)
            pe.wait_ge(sem("wc_in2"), 16)
            pe.wait_ge(sem("wc0"), 1)
            run_steps(pe, 1, 3, lambda s: pro(s, 0, 'c', 'c'))
            run_steps(pe, 3, NC, lambda s: pro(s, 1, 'c', 'c'))
            pe.wait_ge(sem("wl_in"), 16)
            for lo, hi, a in ((NC, NC + 1, (1, 'l', 'c')), (NC + 1, NK, (1, 'l', 'l')),
                              (NK, NK + 1, (1, 0, 'l')), (NK + 1, NK + 3, (1, 0, 0))):
                run_steps(pe, lo, hi, lambda s, a=a: pro(s, *a))

            pe.sem_inc(sem("pv"), 3)

            def q_T(v):
                pe.wait_ge(sem("qst"), v + 1)
                if not isinstance(v, int) or v:
                    pe.wait_ge(sem("c_row"), v)
                for i in range(QB):
                    last = pe.transpose(bT[0:A, 0, i * P:(i + 1) * P], qst[:, i, :], ident[:])
                last.then_inc(sem("qT_mm"), 1)

            def piece(v, h, par, k, banks):
                i, g = divmod(k, NG)
                if k == 0:
                    pe.wait_ge(sem("q2"), v + 1)
                if not (isinstance(v, int) and k < len(banks)):
                    pe.wait_ge(sem("m_red"), NM * v + k + 1 - len(banks))
                pe.matmul(banks[k % len(banks)][:, 0:PIECE], Q2[:, par, i * P:(i + 1) * P],
                          S2[:, h, g * PIECE:(g + 1) * PIECE], start=True, stop=True).then_inc(sem("m_mm"), 1)

            def c_T(v):
                pe.wait_ge(sem("cmax"), v + 1)
                if isinstance(v, int) and v == 0:
                    pe.wait_ge(sem("q1h"), 1)
                    pe.wait_ge(sem("q_lo"), 1)
                else:
                    pe.wait_ge(sem("o_ev"), v)
                for i in range(QB):
                    last = pe.transpose(bT[0:1, 0, i * P:(i + 1) * P], cmax[:, i:i + 1], ident[:])
                last.then_inc(sem("cT_mm"), 1)

            def o_T(v):
                pe.wait_ge(sem("o_cp"), v + 1)
                if not isinstance(v, int):
                    pe.wait_ge(sem("q1h"), v + 2)
                    pe.wait_ge(sem("q_lo"), v + 2)
                else:
                    pe.wait_ge(sem("c_row"), v + 1)
                for i in range(QB):
                    last = pe.transpose(bT[:, 0, i * (D + 1):(i + 1) * (D + 1)], oT_a[0:D + 1, i * P:(i + 1) * P],
                                        ident[0:D + 1, 0:D + 1])
                last.then_inc(sem("oT_a"), 1)

            pe.wait_ge(sem("klo"), NK)
            pe.wait_ge(sem("s1"), NK)
            pe.wait_ge(sem("v_lo"), NK)
            pe.wait_ge(sem("q20"), 1)
            q_T(0)
            for k in range(NM):
                piece(0, 0, 0, k, FIRST_BANKS)
            c_T(0)

            def unit(h, u, j, hn):
                def scores(p):
                    g = NP * u + p
                    sl = (NP * j + p) % 2
                    if p == 0:
                        pe.wait_ge(sem("c_row"), u + 1)
                    pe.wait_ge(sem("exp"), g + 1)
                    for b, c in enumerate(range(2 * p, min(2 * p + 2, NK))):
                        pe.matmul(bS[sl][:, b, :], S1[:, h, c * P:(c + 1) * P], Q1[:, j, :], start=True, stop=False)
                        last = pe.matmul(bS[sl][:, b, :], S2[:, h, c * P:(c + 1) * P], Q2[:, j, :],
                                         start=False, stop=True)
                    last.then_inc(sem("s_mm"), 1)

                def pieces(at):
                    for n in (2 * SLOTS.index(at), 2 * SLOTS.index(at) + 1) if at in SLOTS else ():
                        piece(u + 1, hn, (j + 1) % 2, n, M_BANKS)

                def outputs(p):
                    g = NP * u + p
                    sl = p % 3
                    if p == 0:
                        pe.wait_ge(sem("o_cp"), u + 1)
                    tiles = list(enumerate(range(2 * p, min(2 * p + 2, NK))))
                    pe.wait_ge(sem("p_hi"), g + 1)
                    for b, c in tiles:
                        pe.matmul(bPV[0:D + 1, 0, :], V[:, h % 2, c, 0:D + 1], Ph[:, sl, b, :],
                                  start=c == 0, stop=False, skip_group_check=True)
                        pe.matmul(bPV[0:D, 0, :], V[:, h % 2, c, D + 1:VW], Ph[:, sl, b, :],
                                  start=False, stop=False, skip_group_check=True)
                    pieces((p + 2, 1))
                    if p in POOL_PAIRS:
                        pe.wait_ge(sem("p_lo_g"), len(POOL_PAIRS) * u + POOL_PAIRS.index(p) + 1)
                    else:
                        pe.wait_ge(sem("p_lo"), len(DVE_PAIRS) * u + DVE_PAIRS.index(p) + 1)
                    for b, c in tiles:
                        last = pe.matmul(bPV[0:D + 1, 0, :], V[:, h % 2, c, 0:D + 1],
                                         Pl[:, sl, b, :],
                                         start=False, stop=c == NK - 1, skip_group_check=True)
                    last.then_inc(sem("pv"), 1)

                for p in range(NP):
                    scores(p)
                    if p == 0:
                        q_T(u + 1)
                    pieces((p, 0))
                    if p == 4:
                        o_T(u)
                    if p >= 2:
                        outputs(p - 2)
                    pieces((p, 2))
                c_T(u + 1)
                outputs(NP - 2)
                outputs(NP - 1)

            for h in range(H):
                pe.wait_ge(sem(f"v_in{h % 2}"), 16 * (h // 2) + 16)
                with pe.Fori(0, NB // 2) as i:
                    for j in range(2):
                        hn = h if j == 0 else (h + (i + 1) // (NB // 2)) % H
                        unit(h, NB * h + 2 * i + j, j, hn)
            o_T(UNITS)

            pe.wait_ge(sem("c_wo"), 16)
            pe.wait_ge(sem("c_rt"), 16)

            def fin(s, a, b, c, d):
                if a:
                    pe.wait_ge(sem("ost"), s.v + 1)
                    for k in range(2):
                        last = pe.transpose(bFT[s.par][:, 0, k * P:(k + 1) * P], ost[:, s.par, k * P:(k + 1) * P],
                                            ident[:])
                    last.then_inc(sem("oT_mm"), 1)
                if c:
                    t = s.back(4)
                    pe.wait_ge(sem("x3"), t.v + 1)
                    if not (t.i is None and t.off < 2):
                        pe.wait_ge(sem("x3T"), t.v - 1)
                    for k in range(2):
                        last = pe.transpose(bFX[t.par][:, 0, k * P:(k + 1) * P], x3[:, t.par, k * P:(k + 1) * P],
                                            ident[:])
                    last.then_inc(sem("x3T_mm"), 1)
                if b:
                    t = s.back(1)
                    pe.wait_ge(sem("oT"), t.v + 1)
                    if not (t.i is None and t.off < 2):
                        pe.wait_ge(sem("x2"), t.v - 1)
                    for k in range(2):
                        last = pe.matmul(bFY[t.par][:, 0, 0:DIM], oT[:, t.par, k, :], wot[:, k, :],
                                         start=k == 0, stop=k == 1)
                    last.then_inc(sem("y_mm"), 1)
                if d:
                    t = s.back(5)
                    pe.wait_ge(sem("x3T"), t.v + 1)
                    if not (t.i is None and t.off < 1):
                        pe.wait_ge(sem("lg"), t.v)
                    for k in range(2):
                        last = pe.matmul(bL[:, 0, 0:E], x3T[:, t.par, k, :], rt[:, k, :],
                                         start=k == 0, stop=k == 1)
                    last.then_inc(sem("lg_mm"), 1)

            for lo, hi, a in ((0, 1, (1, 0, 0, 0)), (1, 4, (1, 1, 0, 0)), (4, 5, (1, 1, 1, 0)), (5, NT, (1, 1, 1, 1)),
                              (NT, NT + 1, (0, 1, 1, 1)), (NT + 1, NT + 4, (0, 0, 1, 1)),
                              (NT + 4, NT + 5, (0, 0, 0, 1))):
                run_steps(pe, lo, hi, lambda s, a=a: fin(s, *a))

            pe.wait_ge(sem("M"), 1)
            pe.wait_ge(sem("U"), 1)
            pe.wait_ge(sem("ones"), 1)
            Mf = M[:].rearrange("p t e -> p (t e)")
            pe.matmul(bR[:, 0, 0:P], U[:], Mf, start=True, stop=True)
            pe.matmul(bR[:, 0, P:2 * P], ones[:], Mf, start=False, stop=True, skip_group_check=True)\
                .then_inc(sem("tot_mm"), 1)
            for k in range(2 * NT):
                if k % OHR == 0:
                    pe.wait_ge(sem("ohr"), k // OHR + 1)
                last = pe.matmul(bR[:, 0, 256:256 + 2 * NBLK], ohr[:, k, :], mov[:, k, :, :].rearrange("p a b -> p (a b)"),
                                 start=k == 0, stop=k == 2 * NT - 1)
            last.then_inc(sem("tab_mm"), 1)

            pe.wait_ge(sem("routed"), 1)

            def three(out_ap, st_hi, st_lo, w, e, lo, n, first, last_):
                pe.matmul(out_ap, st_hi, w[:, e, 0, lo:lo + n], start=first, stop=False)
                pe.matmul(out_ap, st_lo, w[:, e, 0, lo:lo + n], start=False, stop=False)
                return pe.matmul(out_ap, st_hi, w[:, e, 1, lo:lo + n], start=False, stop=last_)

            def experts(b):
                v = pe.value_load(eid[0:1, bass.ds(b, 1)], min_val=0, max_val=E ** 3 - 1)
                return v % E, v // E % E, v // (E * E)

            def ffn(s, x_, g, h, eg, eh):
                if h:
                    tb = s.back(2)
                    pe.wait_ge(sem("hs"), tb.v + 1)
                    if not (tb.i is None and tb.off < 1):
                        pe.wait_ge(sem("hlo"), tb.v)
                    for k in range(I // P):
                        last = pe.transpose(bH[:, 0, k * P:(k + 1) * P], hs[:, k * P:(k + 1) * P], ident[:])
                    last.then_inc(sem("hT_mm"), 1)
                if g:
                    t = s.back(1)
                    pe.wait_ge(sem("w_in"), 4 * eg + 4)
                    pe.wait_ge(sem("xlo"), t.v + 1)
                    if not (t.i is None and t.off < 2):
                        pe.wait_ge(sem("hs"), t.v - 1)
                    for k in range(2):
                        last = three(bG[t.par][:, 0, :], xTe[:, t.par, 0, k, :], xTe[:, t.par, 1, k, :], W, eg,
                                     k * 2 * I, I, k == 0, k == 1)
                    last.then_inc(sem("g_mm"), 1)
                    for k in range(2):
                        last = three(bU[t.par][:, 0, :], xTe[:, t.par, 0, k, :], xTe[:, t.par, 1, k, :], W, eg,
                                     k * 2 * I + I, I, k == 0, k == 1)
                    last.then_inc(sem("u_mm"), 1)
                if x_:
                    pe.wait_ge(sem(f"g_in{s.par}"), 16 * s.half + 16)
                    if not (s.i is None and s.off < 1):
                        pe.wait_ge(sem("xlo"), s.v)
                    for k in range(2):
                        last = pe.transpose(bXe[:, 0, k * P:(k + 1) * P], xg[:, s.par, k * P:(k + 1) * P], ident[:])
                    last.then_inc(sem("xTe_mm"), 1)
                if h:
                    pe.wait_ge(sem("hlo"), tb.v + 1)
                    if not (tb.i is None and tb.off < 1):
                        pe.wait_ge(sem("ysb"), tb.v)
                    for k in range(I // P):
                        last = three(bY[:, 0, 0:DIM], hTe[:, 0, k, :], hTe[:, 1, k, :], W, eh,
                                     2 * 2 * I + k * DIM, DIM, k == 0, k == I // P - 1)
                    last.then_inc(sem("y_e"), 1)

            ffn(Step(None, 0), 1, 0, 0, None, None)
            e0, e1, _ = experts(0)
            ffn(Step(None, 1), 1, 1, 0, e0, None)
            ffn(Step(None, 2), 1, 1, 1, e1, e0)
            e1, e2, e3 = experts(1)
            ffn(Step(None, 3), 1, 1, 1, e2, e1)
            ffn(Step(None, 4), 1, 1, 1, e3, e2)
            with pe.Fori(0, (NBLK - 5) // 2) as i:
                eh, eg, en = experts(2 * i + 3)
                ffn(Step(i, 5), 1, 1, 1, eg, eh)
                ffn(Step(i, 6), 1, 1, 1, en, eg)
            eh, eg, _ = experts(NBLK - 2)
            ffn(Step(None, NBLK), 0, 1, 1, eg, eh)
            ffn(Step(None, NBLK + 1), 0, 0, 1, None, eg)


UNITS = H * NB
CTX_LOADS = ((0, 2), (2, NC - 1))
OHR = 4
LAT_AT = 6
SLOTS = [(p, c) for p in range(3, NP - 1) for c in ((0, 2) if p % 2 else (1,))][:NM // 2]
POOL_PAIRS = (2, 4, 6, 8, 10, 12)
DVE_PAIRS = tuple(p for p in range(NP) if p not in POOL_PAIRS)
assert len(SLOTS) == NM // 2

FFN_SEGMENTS = ((0, 1, (1, 0, 0)), (1, 2, (1, 1, 0)), (2, NBLK, (1, 1, 1)), (NBLK, NBLK + 1, (0, 1, 1)),
                (NBLK + 1, NBLK + 2, (0, 0, 1)))


def kernel(**inputs):
    import numpy as np
    import concourse.bacc as bacc
    from concourse.bass_utils import run_bass_kernel_spmd as run

    a = {k.replace("L0_xattn_", "").replace("L0_ffn_", ""): np.asarray(v) for k, v in inputs.items()}
    arrays = {
        "x": a["x"][0], "ctx_in": a["ctx_768"][0], "mask": a["mask_BxS2_bk0"][0],
        "ln_x_g": a["ln_x_g"], "ln_x_b": a["ln_x_b"], "ln_l_g": a["ln_l_g"], "ln_l_b": a["ln_l_b"],
        "qn_g": a["qn_g"], "kn_g": a["kn_g"],
        "w_lat": np.concatenate([a["Wq"], a["Wlkv"]], axis=0).T, "w_ctx": a["Wkv"].T,
        "wo_t": a["Wo"].T, "bo": a["bo"], "router_t": a["router_w"].T, "w13": a["w13"], "w2": a["w2"],
    }
    nc = bacc.Bacc("TRN2", target_bir_lowering=False, num_devices=1)
    args = {}
    for name in arrays:
        arrays[name] = np.ascontiguousarray(arrays[name])
        args[name] = nc.dram_tensor(name, arrays[name].shape, mybir.dt.from_np(arrays[name].dtype),
                                    kind="ExternalInput").ap()
    args["out"] = nc.dram_tensor("out", [TOK + BLK, DIM], F32, kind="ExternalOutput").ap()
    build(nc, **args)
    r = run(nc, [arrays], core_ids=[0])
    return np.asarray(r.results[0]["out"])[0:TOK].reshape(1, TOK, DIM)
```
